# Optimizing a Trainium2 kernel written in Bass

```python
import numpy as np
import jax
import jax.numpy as jnp

def _softmax(x, axis=-1):
    return jax.nn.softmax(x, axis=axis)
def _gelu(x):
    return jax.nn.gelu(x, approximate=True)
def _silu(x):
    return jax.nn.silu(x)
def _sigmoid(x):
    return jax.nn.sigmoid(x)
def _layernorm(x, axis=-1, eps=1e-5):
    m = jnp.mean(x, axis=axis, keepdims=True)
    v = jnp.var(x, axis=axis, keepdims=True)
    return (x - m) / jnp.sqrt(v + eps)
def _scatter_add(tgt, idx, src, axis=0):
    return tgt.at[idx].add(src)
def _segment_sum(src, seg, n):
    return jax.ops.segment_sum(src, seg, n)

kernel_name = 'mk_metaformer_d1_conv_nchw256_225dac'

def setup_inputs(seed: int = 0):
    np.random.seed(seed)
    _w = jnp.asarray
    def _rec_inputs():
        import jax
        import jax.numpy as jnp
        _gk = jax.random.key(seed)
        x = -0.000125 + 0.9999 * jax.random.normal(jax.random.fold_in(_gk, 1), (32, 256, 64, 64), jnp.float32)
        return x
    x = _rec_inputs()
    def _L0_conv_setup():
        import jax, jax.numpy as jnp
        import numpy as np
        K = 2
        LAMBDA_ALPHA = 1.0
        LAMBDA_BETA = 0.5
        key = jax.random.key(seed)
        k1, k2, k3, k4, k5 = jax.random.split(key, 5)
        bs, C, H, W = (32, 256, 64, 64)
        R = 8
        hid = C // R
        x = jax.random.normal(k1, (bs, C, H, W), dtype=jnp.float32)
        w1 = jax.random.normal(k2, (hid, C), dtype=jnp.float32) * 0.05
        b1 = jnp.zeros((hid,), dtype=jnp.float32)
        w2 = jax.random.normal(k3, (K, 2 * C, hid), dtype=jnp.float32) * 0.05
        b2 = jax.random.normal(k4, (K, 2 * C), dtype=jnp.float32) * 0.05
        return {'x': x, 'w1': w1, 'b1': b1, 'w2': w2, 'b2': b2}
    _L0_conv_all = _L0_conv_setup()
    _L0_conv_in = {k: v for k, v in _L0_conv_all.items() if k in ('w1', 'b1', 'w2', 'b2', )}
    del _L0_conv_all

    def _L0_ffn_setup():
        import jax, jax.numpy as jnp
        import numpy as np
        B, S, D = (8, 4096, 256)
        H = 4 * D
        CAPACITY = 0.5
        key = jax.random.key(seed)
        ks = jax.random.split(key, 6)
        x = jax.random.normal(ks[0], (B, S, D), dtype=jnp.float32)
        attention_mask = jnp.zeros((B, 1, 1, S), dtype=jnp.float32)
        wr = jax.random.normal(ks[1], (D, 1), dtype=jnp.float32) * 0.02
        br = jnp.zeros((1,), dtype=jnp.float32)
        w1 = jax.random.normal(ks[2], (D, H), dtype=jnp.float32) * 0.02
        b1 = jnp.zeros((H,), dtype=jnp.float32)
        w2 = jax.random.normal(ks[3], (H, D), dtype=jnp.float32) * 0.02
        b2 = jnp.zeros((D,), dtype=jnp.float32)
        return {'x': x, 'attention_mask': attention_mask, 'wr': wr, 'br': br, 'w1': w1, 'b1': b1, 'w2': w2, 'b2': b2}
    _L0_ffn_all = _L0_ffn_setup()
    _L0_ffn_in = {k: v for k, v in _L0_ffn_all.items() if k in ('attention_mask', 'wr', 'br', 'w1', 'b1', 'w2', 'b2', )}
    del _L0_ffn_all

    return {
        "x": x,
        "L0_conv_w1": _L0_conv_in["w1"],
        "L0_conv_b1": _L0_conv_in["b1"],
        "L0_conv_w2": _L0_conv_in["w2"],
        "L0_conv_b2": _L0_conv_in["b2"],
        "L0_ffn_attention_mask": _L0_ffn_in["attention_mask"],
        "L0_ffn_wr": _L0_ffn_in["wr"],
        "L0_ffn_br": _L0_ffn_in["br"],
        "L0_ffn_w1": _L0_ffn_in["w1"],
        "L0_ffn_b1": _L0_ffn_in["b1"],
        "L0_ffn_w2": _L0_ffn_in["w2"],
        "L0_ffn_b2": _L0_ffn_in["b2"],
    }

def reference(x, L0_conv_w1, L0_conv_b1, L0_conv_w2, L0_conv_b2, L0_ffn_attention_mask, L0_ffn_wr, L0_ffn_br, L0_ffn_w1, L0_ffn_b1, L0_ffn_w2, L0_ffn_b2):
    import jax
    import jax.numpy as jnp
    def _L0_conv_ref(x, w1, b1, w2, b2):
        import jax, jax.numpy as jnp
        import numpy as np
        K = 2
        LAMBDA_ALPHA = 1.0
        LAMBDA_BETA = 0.5
        pooled = x.mean(axis=(2, 3))
        h = jax.nn.relu(pooled @ w1.T + b1)
        delta = 2.0 * jax.nn.sigmoid(jnp.einsum('koh,bh->bko', w2, h) + b2[None]) - 1.0
        alpha = delta[..., 0::2]
        beta = delta[..., 1::2]
        init_alpha = jnp.array([1.0, 0.0], dtype=x.dtype)
        init_beta = jnp.array([1.0, 0.0], dtype=x.dtype)
        a = init_alpha[None, :, None] + LAMBDA_ALPHA * alpha
        b = init_beta[None, :, None] + LAMBDA_BETA * beta
        y = x[:, None] * a[..., None, None] + b[..., None, None]
        return jnp.max(y, axis=1)

    def _L0_ffn_ref(x, attention_mask, wr, br, w1, b1, w2, b2):
        import jax, jax.numpy as jnp
        import numpy as np
        B, S, D = (8, 4096, 256)
        H = 4 * D
        CAPACITY = 0.5
        b, s, d = x.shape
        weights = (jnp.einsum('bsd,do->bso', x, wr) + br)[..., 0]
        k = max(1, int(CAPACITY * s))
        kk = k - 1 if k > 1 else 1
        _, idx = jax.lax.top_k(weights, k)
        sel_idx = idx[:, :kk]
        sel = jnp.take_along_axis(x, sel_idx[:, :, None], axis=1)
        h = jax.nn.gelu(jnp.einsum('bkd,dh->bkh', sel, w1) + b1)
        y = jnp.einsum('bkh,hd->bkd', h, w2) + b2
        w_sel = jnp.take_along_axis(weights, sel_idx, axis=1)
        y = y * w_sel[..., None]
        batch_idx = jnp.arange(b)[:, None]
        processed = jnp.zeros_like(x).at[batch_idx, sel_idx].set(y)
        return processed + x

    def _gn(v, G=32, eps=1e-5):
        B_, C_, H_, W_ = v.shape
        g = v.reshape(B_, G, C_ // G, H_, W_)
        m = jnp.mean(g, axis=(2, 3, 4), keepdims=True)
        s = jnp.var(g, axis=(2, 3, 4), keepdims=True)
        return ((g - m) / jnp.sqrt(s + eps)).reshape(v.shape)

    def _ln_c(v, eps=1e-6):
        m = jnp.mean(v, axis=1, keepdims=True)
        s = jnp.var(v, axis=1, keepdims=True)
        return (v - m) / jnp.sqrt(s + eps)

    def _ln_t(v, eps=1e-5):
        m = jnp.mean(v, axis=-1, keepdims=True)
        s = jnp.var(v, axis=-1, keepdims=True)
        return (v - m) / jnp.sqrt(s + eps)

    def _to_tokens(v):
        B_, C_, H_, W_ = v.shape
        return v.reshape(B_, C_, H_ * W_).transpose(0, 2, 1)
    def _from_tokens(t, like):
        B_, C_, H_, W_ = like.shape
        return t.transpose(0, 2, 1).reshape(B_, C_, H_, W_)

    x = x + _L0_conv_ref(_ln_c(x), L0_conv_w1, L0_conv_b1, L0_conv_w2, L0_conv_b2)
    t = _to_tokens(x)
    t = t + _L0_ffn_ref(_ln_t(t), L0_ffn_attention_mask, L0_ffn_wr, L0_ffn_br, L0_ffn_w1, L0_ffn_b1, L0_ffn_w2, L0_ffn_b2)
    x = _from_tokens(t, x)
    return x


_drawn_inputs = setup_inputs


def setup_inputs(seed=0):
    import zlib

    import numpy as np

    out = dict(_drawn_inputs(seed))
    spreads = {'L0_conv_b1': (0.0, 0.8), 'L0_ffn_b1': (0.0, 0.8), 'L0_ffn_b2': (0.0, 0.8)}
    factors = {'L0_conv_w1': 8.0,
     'L0_conv_w2': 8.0,
     'L0_conv_b2': 4.316,
     'L0_ffn_wr': 5.84,
     'L0_ffn_w1': 6.815,
     'L0_ffn_w2': 6.354}
    for name, (base, spread) in spreads.items():
        noise = np.random.default_rng([zlib.crc32(name.encode()), seed]).standard_normal(out[name].shape)
        drawn = base * np.exp(spread * noise) if base else spread * noise
        out[name] = jnp.asarray(drawn.astype(out[name].dtype))
    for name, factor in factors.items():
        out[name] = (out[name] * factor).astype(out[name].dtype)
    return out
```

```python
from contextlib import ExitStack

from concourse import mybir
from concourse.bass import IndirectOffsetOnAxis

ALU = mybir.AluOpType
ACT = mybir.ActivationFunctionType
F32 = mybir.dt.float32
F32R = mybir.dt.float32r
BF16 = mybir.dt.bfloat16
I32 = mybir.dt.int32
U32 = mybir.dt.uint32
AX_X = mybir.AxisListType.X

P = 128
DMA = 16
LAG = 2
G_RING = 4
AUX = 3
EPS_C = 1e-6
EPS_T = 1e-5


def plan(blocks, steps):
    at = {s: [] for s in range(steps)}

    def put(s, *jobs):
        at[s].extend(jobs)

    chunks = blocks // 4
    for i, c in enumerate(range(3, chunks)):
        put(2 + i, ("FN", -1, c))
    for g in range(8):
        put(g // 2, ("N1", 1, g))
    put(4, ("N1norm", 1, 0))
    for g in range(8, 16):
        put(5 + (g - 8) // 2, ("N1", 1, g))
    put(9, ("N1norm", 1, 1))
    put(10, ("SE1", 1, 0))
    put(11, ("SE2", 1, 0))
    for k in range(chunks):
        put(12 + k, ("CV", 1, k))
        put(13 + k, ("N2", 1, k))
        if k == 3:
            put(13 + k, ("N2norm", 1, 0))
    put(20, ("N2norm", 1, 1))
    put(21, ("TKkeys", 1, 0))
    for r in range(4):
        put(21 + r, ("TK", 1, r))
    put(25, ("TKlow", 1, 0))
    for r in range(4, 8):
        put(21 + r, ("TK", 1, r))
    put(29, ("RANK", 1, 0))
    for c in range(3):
        put(13 + 8 * c, ("FN", 0, c))
    return at


def bank_uses(steps_of_chunk, steps, plan_, ffn, prev, ahead):
    uses, n = {}, 0
    many = {"N1": 1, "N2": 2, "CV": 2, "FN": 2}
    for s in range(steps):
        if ffn and s % steps_of_chunk == 0:
            uses["XS", 0, s // steps_of_chunk] = n
            n += 2
        for job in jobs_at(plan_, s, ffn, prev, ahead):
            if job[0] in many:
                uses[job] = n
                n += many[job[0]]
    return uses, n


def jobs_at(plan_, s, ffn, prev, ahead):
    there = {-1: prev, 0: ffn, 1: ahead}
    return [job for job in plan_[s] if there[job[1]]]


def metaformer_kernel(nc, x, conv_w1, conv_b1, conv_w2, conv_b2, router_w, router_b, ffn_w1, ffn_b1,
                      ffn_w2, ffn_b2, consts, out):
    IMAGES, C, TOKENS = x.shape
    H = ffn_w1.shape[1]
    HALVES = C // P
    BLOCKS = TOKENS // P
    CHUNK = 512
    CHUNKS = TOKENS // CHUNK
    SLOTS = TOKENS // 2
    CHOSEN = SLOTS - 1
    FCHUNKS = SLOTS // CHUNK
    HB = H // P
    STEPS = FCHUNKS * HB
    GROUP = 16
    KGROUPS = 4
    RELU_H = P // KGROUPS
    DIGITS = 15
    ROUNDS = 8
    assert IMAGES % 2 == 0 and IMAGES >= 4
    PLAN = plan(BLOCKS, STEPS)

    xT = x.rearrange("b (h p) t -> b p h t", p=P)
    oT = out.rearrange("b (h p) t -> b p h t", p=P)

    ctx = ExitStack()
    with ctx:
        def sb(name, shape, dt):
            return ctx.enter_context(nc.sbuf_tensor(name, shape, dt))

        def sem(name):
            return ctx.enter_context(nc.semaphore(name))

        X = [sb(f"X{q}", [P, HALVES, TOKENS], F32) for q in range(2)]
        T = [sb(f"T{q}", [P, BLOCKS, C], F32) for q in range(2)]
        w1_hi = sb("w1_hi", [P, HALVES, H], F32R)
        w1_lo = sb("w1_lo", [P, HALVES, H], F32R)
        w2_hi = sb("w2_hi", [P, HB, C], F32R)
        w2_lo = sb("w2_lo", [P, HB, C], F32R)
        g_hi = [sb(f"g_hi{r}", [P, CHUNK], F32R) for r in range(G_RING)]
        g_lo = [sb(f"g_lo{r}", [P, CHUNK], F32R) for r in range(G_RING)]
        rows = sb("rows", [P, 4, C], F32)
        xs_hi = sb("xs_hi", [P, HALVES, CHUNK], F32R)
        xs_lo = sb("xs_lo", [P, HALVES, CHUNK], F32R)
        y_rows = sb("y_rows", [P, 4, C], F32)
        y_back = sb("y_back", [P, 8, C], F32)
        branch = [sb(f"branch{r}", [P, CHUNK], F32) for r in range(2)]
        ident = sb("ident", [P, P], F32)
        tri_f = sb("tri_f", [P, P], F32)
        tri = sb("tri", [P, P], BF16)
        digits = sb("digits", [P, DIGITS], F32)
        ones_f = sb("ones_f", [P, P], F32)
        ones_b = sb("ones_b", [P, P], BF16)
        cw1 = sb("cw1", [P, HALVES, P], F32)
        cb1 = sb("cb1", [P, 1], F32)
        cw2 = sb("cw2", [P, C], F32)
        cb2 = sb("cb2", [P, HALVES, KGROUPS], F32)
        rw = sb("rw", [P, HALVES], F32)
        rb = sb("rb", [P, 1], F32)
        rw_sum = sb("rw_sum", [P, 1], F32)
        fb1 = sb("fb1", [P, HB], F32)
        fb2 = sb("fb2", [P, C], F32)
        stats = sb("stats", [P, GROUP, 6], F32)
        tmp = [sb(f"tmp{i}", [P, BLOCKS], F32) for i in range(4)]
        mean = sb("mean", [P, BLOCKS], F32)
        rstd = sb("rstd", [P, BLOCKS], F32)
        pooled = sb("pooled", [P, HALVES], F32)
        hid = sb("hid", [P, 1], F32)
        group_mask = sb("group_mask", [P, KGROUPS], F32)
        hid4 = sb("hid4", [P, KGROUPS], F32)
        pre = sb("pre", [P, HALVES, KGROUPS], F32)
        delta = sb("delta", [P, HALVES, KGROUPS], F32)
        coef = sb("coef", [P, HALVES, KGROUPS], F32)
        logit = [sb(f"logit{q}", [P, BLOCKS], F32) for q in range(2)]
        index = [sb(f"index{q}", [P, BLOCKS], U32) for q in range(2)]
        flip = sb("flip", [P, BLOCKS], U32)
        key = sb("key", [P, BLOCKS], U32)
        key_hi = sb("key_hi", [P, BLOCKS], U32)
        key_lo = sb("key_lo", [P, BLOCKS], U32)
        digit_key = sb("digit_key", [P, BLOCKS], F32)
        low_key = sb("low_key", [P, BLOCKS], F32)
        base = [sb(f"base{i}", [P, 1], F32) for i in range(2)]
        tried = sb("tried", [P, DIGITS], F32)
        above = sb("above", [P, DIGITS, BLOCKS], BF16)
        count = sb("count", [P, DIGITS], BF16)
        junk = sb("junk", [P, DIGITS], F32)
        passed = sb("passed", [P, 1], F32)
        gt_eq = sb("gt_eq", [P, 2, BLOCKS], BF16)
        incl = [sb(f"incl{i}", [P, BLOCKS], F32) for i in range(2)]
        before = [sb(f"before{i}", [P, BLOCKS], F32) for i in range(2)]
        need = sb("need", [P, 1], F32)
        chosen = sb("chosen", [P, BLOCKS], F32)
        ones_row = sb("ones_row", [P, BLOCKS], F32)

        psum = [ctx.enter_context(nc.psum_tensor(f"psum{i}", [P, 512], F32)) for i in range(8)]
        y_ps, h_ps, aux_ps, small = psum[0:2], psum[2:4], psum[4:4 + AUX], psum[7]
        POOL_COL, LOGIT_COL, SE_COL, CNT_COL, RANK_COL = 0, 64, 96, 112, 128
        RWS_COL = 300
        x_table = [nc.dram_tensor(f"x_table{q}", (SLOTS, C), F32).ap() for q in range(2)]
        y_table = [nc.dram_tensor(f"y_table{q}", (SLOTS, C), F32).ap() for q in range(2)]

        s_const = sem("s_const")
        s_met = sem("s_met")
        s_wload = sem("s_wload")
        s_zero = sem("s_zero")
        s_zrow = sem("s_zrow")
        s_wsplit = sem("s_wsplit")
        s_rws = sem("s_rws")
        s_xin = [sem(f"s_xin{k}") for k in range(CHUNKS)]
        s_out = [sem(f"s_out{k}") for k in range(CHUNKS)]
        s_tok = sem("s_tok")
        s_copied = sem("s_copied")
        s_norm = sem("s_norm")
        s_pool = sem("s_pool")
        s_pooled = sem("s_pooled")
        s_hid = sem("s_hid")
        s_hidr = sem("s_hidr")
        s_se = sem("s_se")
        s_pre = sem("s_pre")
        s_delta = sem("s_delta")
        s_coef = sem("s_coef")
        s_cv = sem("s_cv")
        s_branch = sem("s_branch")
        s_logit = sem("s_logit")
        s_cnt = sem("s_cnt")
        s_tot = sem("s_tot")
        s_index = sem("s_index")
        s_scat = sem("s_scat")
        s_rows = sem("s_rows")
        s_xs = sem("s_xs")
        s_xshi = sem("s_xshi")
        s_h = sem("s_h")
        s_g = sem("s_g")
        s_glo = sem("s_glo")
        s_mm2 = sem("s_mm2")
        s_y = sem("s_y")
        s_ytab = [sem(f"s_ytab{f}") for f in range(FCHUNKS)]
        s_back = [sem(f"s_back{i}") for i in range(2)]
        s_scaled = sem("s_scaled")
        s_fn = sem("s_fn")
        s_hid4 = sem("s_hid4")
        s_aux = sem("s_aux")
        s_chain = sem("s_chain")


        block = ctx.enter_context(nc.Block())
        CHAIN = {}

        class Period:

            def __init__(self, b, q, ffn, prev, ahead, banks_before):
                self.b, self.q, self.ffn, self.prev, self.ahead = b, q, ffn, prev, ahead
                self.uses, self.n_uses = bank_uses(HB, STEPS, PLAN, ffn, prev, ahead)
                self.before = banks_before

            def image(self, off):
                return self.b + off, self.q ^ (off & 1)

            def jobs(self, s):
                return jobs_at(PLAN, s, self.ffn, self.prev, self.ahead)

            def use(self, job, k=0):
                n = self.uses[job] + k
                phase = self.before[1] + n
                return aux_ps[phase % AUX], self.before[0] + n

        full = bank_uses(HB, STEPS, PLAN, True, True, True)[1]
        fill0 = bank_uses(HB, STEPS, PLAN, False, False, True)[1]
        fill1 = bank_uses(HB, STEPS, PLAN, True, False, True)[1]
        last = bank_uses(HB, STEPS, PLAN, True, True, False)[1]
        assert full % AUX == 0

        def run(eng, period):
            steady = fill0 + fill1 - full
            period(Period(-1, 1, False, False, True, (0, 0)))
            period(Period(0, 0, True, False, True, (fill0, fill0)))
            period(Period(1, 1, True, True, True, (full + steady, full + steady)))
            with eng.Fori(0, (IMAGES - 4) // 2) as i:
                for n in range(2):
                    b = 2 * i + (2 + n)
                    period(Period(b, n, True, True, True, (full * b + steady, full + steady)))
            b = IMAGES - 2
            period(Period(b, 0, True, True, True, (full * b + steady, full + steady)))
            b = IMAGES - 1
            period(Period(b, 1, True, True, False, (full * b + steady, full + steady)))
            period(Period(IMAGES, 0, False, True, False, (full * b + steady + last, full + steady + last)))

        def settled(eng):
            eng.sem_inc(s_met, 1)

        def tokens(k, n=CHUNK):
            return slice(k * n, (k + 1) * n)

        @block.sync
        def _(sp):
            for dst, src in ((ident, consts[:, 0:P]), (tri_f, consts[:, P:2 * P]),
                             (digits, consts[:, 2 * P:2 * P + DIGITS]),
                             (group_mask, consts[:, 2 * P + DIGITS:2 * P + DIGITS + KGROUPS]),
                             (cw1, conv_w1.rearrange("(h p) m -> p h m", p=P)), (cb1, conv_b1),
                             (cw2, conv_w2), (cb2, conv_b2), (rw, router_w), (rb, router_b),
                             (fb1, ffn_b1), (fb2, ffn_b2)):
                sp.dma_start(dst[:], src).then_inc(s_const, DMA)
            sp.dma_start(T[1][:, 0:8, :].rearrange("p (h m) c -> p h (m c)", h=HALVES),
                         ffn_w1.rearrange("(h p) m -> p h m", p=P)).then_inc(s_wload, DMA)
            sp.dma_start(T[1][:, 8:16, :], ffn_w2.rearrange("(h p) m -> p h m", p=P)).then_inc(s_wload, DMA)
            for b in range(2):
                for k in range(CHUNKS):
                    if b:
                        sp.wait_ge(s_xin[k], DMA)
                    sp.dma_start(X[b][:, :, tokens(k)], xT[b, :, :, tokens(k)]).then_inc(s_xin[k], DMA)
            sp.wait_ge(s_zero, 2)
            for q in range(2):
                sp.dma_start(x_table[q][SLOTS - 1:SLOTS, :], y_back[0:1, 0, :]).then_inc(s_zrow, DMA)
            sp.wait_ge(s_zrow, 2 * DMA)

            def period(p):
                reload = {}
                if p.ffn:
                    sp.wait_ge(s_scat, DMA * BLOCKS * (p.b + 1))
                    settled(sp)
                    sp.dma_start(rows[:], x_table[p.q][0:CHUNK, :].rearrange("(p i) c -> p i c", i=4)
                                 ).then_inc(s_rows, DMA)
                for s in range(STEPS):
                    if s % HB == 1 and (p.ffn if s > HB else p.prev):
                        f, (b, q) = ((s - HB) // HB, p.image(0)) if s > HB else (FCHUNKS - 1, p.image(-1))
                        sp.wait_ge(s_y, FCHUNKS * b + f + 1)
                        settled(sp)
                        sp.dma_start(y_table[q][f * CHUNK:(f + 1) * CHUNK, :].rearrange("(p i) c -> p i c", i=4),
                                     y_rows[:]).then_inc(s_ytab[f], DMA)
                    for c, b, q in reload.pop(s, []):
                        sp.wait_ge(s_out[c], DMA * (b + 1))
                        settled(sp)
                        sp.dma_start(X[q][:, :, tokens(c)], xT[b + 2, :, :, tokens(c)]).then_inc(s_xin[c], DMA)
                    for job in p.jobs(s):
                        if job[0] == "FN":
                            c, (b, q) = job[2], p.image(job[1])
                            sp.wait_ge(s_aux, p.use(job, 1)[1] + 1)
                            settled(sp)
                            sp.dma_start(oT[b, :, :, tokens(c)], X[q][:, :, tokens(c)]).then_inc(s_out[c], DMA)
                            if (p.ahead if job[1] else not (type(p.b) is int and p.b + 2 >= IMAGES)):
                                reload.setdefault(s + 1, []).append((c, b, q))
                assert not reload

            run(sp, period)
            for k in range(CHUNKS):
                sp.wait_ge(s_out[k], DMA * IMAGES)

        @block.gpsimd
        def _(pool):
            nc.gpsimd.memset(y_back[:], 0.0).then_inc(s_zero, 1)

            def period(p):
                for s in range(STEPS):
                    for job in p.jobs(s):
                        b, q = p.image(job[1])
                        if job[0] == "FN":
                            c = job[2]
                            known = min(CHUNK * (c + 1), SLOTS)
                            pool.wait_ge(s_ytab[min(c, FCHUNKS - 1)], DMA * (b + 1))
                            settled(pool)
                            if type(b) is not int or 2 * HALVES * 4 * b + 2 * c - 2 > 0:
                                pool.wait_ge(s_fn, 2 * CHUNKS * b + 2 * c - 2)
                                settled(pool)
                            for i in range(4):
                                j = 4 * c + i
                                pool.indirect_dma_start(
                                    y_back[:, 4 * (c % 2) + i, :], None, y_table[q][0:known, :],
                                    IndirectOffsetOnAxis(ap=index[q][:, j:j + 1], axis=0),
                                    bounds_check=min(known, CHOSEN) - 1, oob_is_err=False).then_inc(s_back[c % 2], DMA)
                        elif job[0] == "RANK":
                            pool.wait_ge(s_index, b + 1)
                            settled(pool)
                            for j in range(BLOCKS):
                                pool.indirect_dma_start(
                                    x_table[q], IndirectOffsetOnAxis(ap=index[q][:, j:j + 1], axis=0),
                                    T[q][:, j, :], None,
                                    bounds_check=CHOSEN - 1, oob_is_err=False).then_inc(s_scat, DMA)

            run(pool, period)

        @block.tensor
        def _(pe):
            pe.wait_ge(s_const, DMA * 12)
            pe.wait_ge(s_wsplit, 1)
            for h in range(HALVES):
                rws = nc.tensor.matmul(small[:, RWS_COL:RWS_COL + 1], ones_f[:], rw[:, h:h + 1],
                                       start=(h == 0), stop=(h == HALVES - 1))
            rws.then_inc(s_rws, 1)

            def flip_block(out, src, **flags):
                return nc.tensor.matmul(out, src, ident[:], is_transpose=True, skip_group_check=True, **flags)

            def bank_of(p, job, k=0):
                bank, n = p.use(job, k)
                if type(n) is not int or n >= AUX:
                    pe.wait_ge(s_aux, n - (AUX - 1))
                return bank

            def to_tokens(p, job, k, q, pair):
                bank = bank_of(p, job, k)
                for i in range(2):
                    for h in range(HALVES):
                        t = flip_block(bank[:, i * C + h * P:i * C + (h + 1) * P],
                                       X[q][:, h, tokens(2 * pair + i, P)], start=(i + h == 0), stop=True)
                t.then_inc(s_tok, 1)

            def stage(p, job):
                kind, off, k = job
                b, q = p.image(off)
                if kind == "N1":
                    if k % 2 == 0:
                        pe.wait_ge(s_xin[k // 2], DMA * (b + 1))
                    to_tokens(p, job, 0, q, k)
                elif kind == "N1norm":
                    pe.wait_ge(s_norm, 4 * b + k + 1)
                    for j in range(GROUP * k, GROUP * (k + 1)):
                        for h in range(HALVES):
                            col = POOL_COL + h * BLOCKS + j
                            m = nc.tensor.matmul(small[:, col:col + 1], T[q][:, j, h * P:(h + 1) * P],
                                                 ones_f[:, 0:1], start=True, stop=True)
                    if k == 1:
                        m.then_inc(s_pool, 1)
                elif kind == "SE1":
                    pe.wait_ge(s_pooled, b + 1)
                    for h in range(HALVES):
                        m = nc.tensor.matmul(small[:, SE_COL:SE_COL + 1], cw1[:, h, :], pooled[:, h:h + 1],
                                             start=(h == 0), stop=(h == HALVES - 1))
                    m.then_inc(s_hid, 1)
                elif kind == "SE2":
                    pe.wait_ge(s_hid4, b + 1)
                    for h in range(HALVES):
                        col = SE_COL + 1 + KGROUPS * h
                        m = nc.tensor.matmul(small[:, col:col + KGROUPS], cw2[:, h * P:(h + 1) * P], hid4[:],
                                             start=True, stop=True)
                    m.then_inc(s_se, 1)
                elif kind == "CV":
                    for h in range(HALVES):
                        bank = bank_of(p, job, h)
                        for i in range(4):
                            t = flip_block(bank[:, tokens(i, P)], T[q][:, 4 * k + i, h * P:(h + 1) * P],
                                           start=(i == 0), stop=True)
                        t.then_inc(s_cv, 1)
                elif kind == "N2":
                    pe.wait_ge(s_aux, p.use(("CV", off, k), 1)[1] + 1)
                    for i in range(2):
                        to_tokens(p, job, i, q, 2 * k + i)
                    for j in range(4 * k, 4 * k + 4):
                        for h in range(HALVES):
                            m = nc.tensor.matmul(small[:, LOGIT_COL + j:LOGIT_COL + j + 1],
                                                 X[q][:, h, tokens(j, P)], rw[:, h:h + 1],
                                                 start=(h == 0), stop=(h == HALVES - 1))
                    m.then_inc(s_logit, 1)
                elif kind == "TK":
                    pe.wait_ge(s_cnt, (ROUNDS + 1) * b + k + 1)
                    nc.tensor.matmul(small[:, CNT_COL:CNT_COL + DIGITS], ones_b[:], count[:],
                                     start=True, stop=True).then_inc(s_tot, 1)
                elif kind == "RANK":
                    pe.wait_ge(s_cnt, (ROUNDS + 1) * (b + 1))
                    both = gt_eq[:].rearrange("p a j -> p (a j)")
                    nc.tensor.matmul(small[:, RANK_COL:RANK_COL + 2 * BLOCKS], tri[:], both,
                                     start=True, stop=True)
                    nc.tensor.matmul(small[:, RANK_COL + 2 * BLOCKS:RANK_COL + 4 * BLOCKS], ones_b[:], both,
                                     start=True, stop=True).then_inc(s_tot, 1)
                elif kind == "FN":
                    pe.wait_ge(s_scaled, CHUNKS * b + k + 1)
                    for h in range(HALVES):
                        bank = bank_of(p, job, h)
                        for i in range(4):
                            flip_block(bank[:, tokens(i, P)], T[q][:, 4 * k + i, h * P:(h + 1) * P],
                                       start=(i == 0), stop=False)
                        for i in range(4):
                            t = flip_block(bank[:, tokens(i, P)], y_back[:, 4 * (k % 2) + i, h * P:(h + 1) * P],
                                           start=False, stop=True)
                        t.then_inc(s_fn, 1)

            def first_product(p, s):
                h, bank = s % HB, h_ps[s % 2]
                if s % HB == 0:
                    pe.wait_ge(s_aux, p.use(("XS", 0, s // HB), 1)[1] + 1)
                if s >= 2 or p.prev:
                    pe.wait_ge(s_glo, STEPS * p.b + s - 1)
                n = 0
                for half in range(HALVES):
                    for w, v in ((w1_hi, xs_hi), (w1_lo, xs_hi), (w1_hi, xs_lo)):
                        m = nc.tensor.matmul(bank[:], w[:, half, h * P:(h + 1) * P], v[:, half, :],
                                             start=(n == 0), stop=(n == 5))
                        n += 1
                m.then_inc(s_h, 1)

            def second_product(b, s):
                h, f, r = s % HB, s // HB, s % G_RING
                pe.wait_ge(s_glo, STEPS * b + s + 1)
                if h == 0 and (type(b) is not int or FCHUNKS * b + f > 0):
                    pe.wait_ge(s_y, FCHUNKS * b + f)
                for i in range(4):
                    for n, (g, w) in enumerate(((g_hi, w2_hi), (g_lo, w2_hi), (g_hi, w2_lo))):
                        m = nc.tensor.matmul(y_ps[i // 2][:, (i % 2) * C:(i % 2 + 1) * C],
                                             g[r][:, tokens(i, P)], w[:, h, :],
                                             start=(h == 0 and n == 0 and i % 2 == 0),
                                             stop=(h == HB - 1 and n == 2), skip_group_check=True)
                if h == HB - 1:
                    m.then_inc(s_mm2, 1)

            def period(p):
                for s in range(STEPS):
                    if p.ffn and s % HB == 0:
                        f = s // HB
                        pe.wait_ge(s_rows, DMA * (FCHUNKS * p.b + f + 1))
                        for h in range(HALVES):
                            bank = bank_of(p, ("XS", 0, f), h)
                            for i in range(4):
                                t = flip_block(bank[:, tokens(i, P)], rows[:, i, h * P:(h + 1) * P],
                                               start=(i == 0), stop=True)
                            t.then_inc(s_xs, 1)
                    if p.ffn:
                        first_product(p, s)
                    for job in p.jobs(s):
                        stage(p, job)
                    if s < LAG and p.prev:
                        second_product(p.b - 1, STEPS + s - LAG)
                    if s >= LAG and p.ffn:
                        second_product(p.b, s - LAG)

            run(pe, period)

        @block.scalar
        def _(act):
            def stage(p, job):
                kind, off, k = job
                b, q = p.image(off)
                if kind in ("N1", "N2"):
                    for i in range(1 if kind == "N1" else 2):
                        n = k if kind == "N1" else 2 * k + i
                        act.wait_ge(s_tok, BLOCKS * b + (0 if kind == "N1" else BLOCKS // 2) + n + 1)
                        nc.scalar.copy(T[q][:, 2 * n:2 * n + 2, :].rearrange("p j c -> p (j c)"),
                                       p.use(job, i)[0][:]).then_inc(s_copied, 1)
                elif kind == "SE1":
                    act.wait_ge(s_hid, b + 1)
                    nc.scalar.activation(hid[:], small[:, SE_COL:SE_COL + 1], ACT.Relu, bias=cb1[:, 0:1],
                                         scale=1.0 / TOKENS).then_inc(s_hidr, 1)
                elif kind == "SE2":
                    act.wait_ge(s_pre, b + 1)
                    nc.scalar.activation(delta[:], pre[:], ACT.Tanh, scale=0.5).then_inc(s_delta, 1)
                elif kind == "CV":
                    if k == 0:
                        act.wait_ge(s_coef, b + 1)
                    for h in range(HALVES):
                        act.wait_ge(s_cv, 2 * CHUNKS * b + 2 * k + h + 1)
                        if k:
                            act.wait_ge(s_aux, p.use((kind, off, k - 1), h)[1] + 1)
                        nc.scalar.activation(branch[h][:], p.use(job, h)[0][:], ACT.Identity,
                                             bias=coef[:, h, 3:4], scale=coef[:, h, 2:3]).then_inc(s_branch, 1)
                elif kind == "FN":
                    act.wait_ge(s_back[k % 2], DMA * 4 * (CHUNKS // 2 * b + k // 2 + 1))
                    for i in range(4):
                        row = y_back[:, 4 * (k % 2) + i, :]
                        a = nc.scalar.activation(row, row, ACT.Identity, scale=logit[q][:, 4 * k + i:4 * k + i + 1])
                    a.then_inc(s_scaled, 1)

            def period(p):
                for s in range(STEPS):
                    if p.ffn and s % HB == 0:
                        f = s // HB
                        for h in range(HALVES):
                            act.wait_ge(s_xs, 2 * FCHUNKS * p.b + 2 * f + h + 1)
                            nc.scalar.copy(xs_hi[:, h, :], p.use(("XS", 0, f), h)[0][:]).then_inc(s_xshi, 1)
                        if f + 1 < FCHUNKS:
                            act.dma_start(rows[:], x_table[p.q][(f + 1) * CHUNK:(f + 2) * CHUNK, :]
                                          .rearrange("(p i) c -> p i c", i=4)).then_inc(s_rows, DMA)
                    if p.ffn:
                        act.wait_ge(s_h, STEPS * p.b + s + 1)
                        bank, h = h_ps[s % 2], s % HB
                        nc.scalar.activation(g_hi[s % G_RING][:], bank[:], ACT.Gelu_apprx_tanh, bias=fb1[:, h:h + 1])
                        nc.scalar.activation(bank[:], bank[:], ACT.Gelu_apprx_tanh,
                                             bias=fb1[:, h:h + 1]).then_inc(s_g, 1)
                    for job in p.jobs(s):
                        stage(p, job)
                if p.ahead and type(p.b) is int and p.b == -1:
                    act.wait_ge(s_wsplit, 2)

            act.wait_ge(s_const, DMA * 12)
            run(act, period)

        @block.vector
        def _(dve):
            links = [0]

            def link(ins, b=0):
                links[0] += 1
                ins.then_inc(s_chain, 1)
                dve.wait_ge(s_chain, CHAIN.get("setup", 0) + CHAIN.get("image", 0) * b + links[0])

            nc.vector.memset(ones_f[:], 1.0)
            nc.vector.memset(ones_row[:], 1.0)
            nc.vector.memset(ones_b[:], 1.0).then_inc(s_zero, 1)
            dve.wait_ge(s_const, DMA * 12)
            nc.vector.tensor_copy(tri[:], tri_f[:]).then_inc(s_wsplit, 1)
            dve.wait_ge(s_rws, 1)
            link(nc.vector.tensor_scalar(rw_sum[:], small[:, RWS_COL:RWS_COL + 1], -1.0, None, ALU.mult))
            dve.wait_ge(s_wload, 2 * DMA)
            w1_raw = T[1][:, 0:8, :].rearrange("p (h m) c -> p h (m c)", h=HALVES)
            w2_raw = T[1][:, 8:16, :]
            nc.vector.tensor_copy(w1_hi[:], w1_raw)
            link(nc.vector.tensor_copy(w2_hi[:], w2_raw))
            nc.vector.tensor_tensor(w1_lo[:], w1_raw, w1_hi[:].bitcast(F32), ALU.subtract)
            nc.vector.tensor_tensor(w2_lo[:], w2_raw, w2_hi[:].bitcast(F32), ALU.subtract).then_inc(s_wsplit, 1)
            CHAIN["setup"], links[0] = links[0], 0

            def block_stats(p, job, k, b, q, pair, copied):
                dve.wait_ge(s_copied, BLOCKS * b + copied + 1)
                j = 2 * pair
                nc.vector.bn_stats(stats[:, j % GROUP, :], T[q][:, j, :]).then_inc(s_aux, 1)
                ins = nc.vector.bn_stats(stats[:, (j + 1) % GROUP, :], T[q][:, j + 1, :])
                if (j + 2) % GROUP == 0:
                    link(ins, b)

            def norm(b, q, g, eps):
                js = slice(GROUP * g, GROUP * (g + 1))
                a, d, v, u = (t[:, 0:GROUP] for t in tmp)
                m, r = mean[:, js], rstd[:, js]
                nc.vector.tensor_tensor(d, stats[:, :, 1], stats[:, :, 4], ALU.subtract)
                nc.vector.tensor_tensor(a, stats[:, :, 1], stats[:, :, 4], ALU.add)
                link(nc.vector.tensor_tensor(v, stats[:, :, 2], stats[:, :, 5], ALU.add), b)
                nc.vector.tensor_scalar(m, a, 0.5, None, ALU.mult)
                link(nc.vector.tensor_tensor(u, d, d, ALU.mult), b)
                link(nc.vector.scalar_tensor_tensor(a, u, C / 4.0, v, ALU.mult, ALU.add), b)
                link(nc.vector.tensor_scalar(v, a, 1.0 / C, eps, ALU.mult, ALU.add), b)
                link(nc.vector.tensor_scalar(r.bitcast(I32), v.bitcast(I32), -0.5, 1597463007.0, ALU.mult, ALU.add), b)
                for _ in range(3):
                    link(nc.vector.tensor_tensor(a, r, r, ALU.mult), b)
                    link(nc.vector.scalar_tensor_tensor(u, a, -0.5, v, ALU.mult, ALU.mult), b)
                    link(nc.vector.scalar_tensor_tensor(r, u, 1.5, r, ALU.add, ALU.mult), b)
                for j in range(GROUP * g, GROUP * (g + 1)):
                    ins = nc.vector.tensor_scalar(T[q][:, j, :], T[q][:, j, :], mean[:, j:j + 1],
                                                  rstd[:, j:j + 1], ALU.subtract, ALU.mult)
                ins.then_inc(s_norm, 1)

            def digit_found(b, k):
                dve.wait_ge(s_tot, (ROUNDS + 1) * b + k + 1)
                link(nc.vector.tensor_scalar(junk[:], small[:, CNT_COL:CNT_COL + DIGITS], float(CHOSEN), None,
                                             ALU.is_ge, ALU.add, accum_out=passed[:]), b)
                link(nc.vector.scalar_tensor_tensor(base[(k + 1) % 2][:], passed[:], 16.0 ** (3 - k % 4),
                                                    base[k % 2][:], ALU.mult, ALU.add), b)

            def stage(p, job):
                kind, off, k = job
                b, q = p.image(off)
                if kind == "N1":
                    block_stats(p, job, 0, b, q, k, k)
                elif kind == "N1norm":
                    norm(b, q, k, EPS_C)
                elif kind == "SE1":
                    dve.wait_ge(s_pool, b + 1)
                    nc.vector.tensor_reduce(
                        pooled[:], small[:, POOL_COL:POOL_COL + 2 * BLOCKS].rearrange("p (h j) -> p h j", h=HALVES),
                        AX_X, ALU.add).then_inc(s_pooled, 1)
                    dve.wait_ge(s_hidr, b + 1)
                    nc.vector.tensor_scalar(hid4[:], group_mask[:], hid[:, 0:1], None, ALU.mult).then_inc(s_hid4, 1)
                elif kind == "SE2":
                    dve.wait_ge(s_se, b + 1)
                    nc.vector.tensor_tensor(
                        pre[:], small[:, SE_COL + 1:SE_COL + 1 + 2 * KGROUPS].rearrange("p (h k) -> p h k", h=HALVES),
                        cb2[:], ALU.add).then_inc(s_pre, 1)
                    dve.wait_ge(s_delta, b + 1)
                    nc.vector.tensor_scalar(coef[:, :, 0], delta[:, :, 0], 1.0, None, ALU.add)
                    nc.vector.tensor_copy(coef[:, :, 2], delta[:, :, 2])
                    link(nc.vector.tensor_scalar(coef[:, :, 1], delta[:, :, 1], 0.5, 1.0, ALU.mult, ALU.add), b)
                    nc.vector.scalar_tensor_tensor(coef[:, :, 3], delta[:, :, 3], 0.5, coef[:, :, 1],
                                                   ALU.mult, ALU.subtract).then_inc(s_coef, 1)
                elif kind == "CV":
                    for h in range(HALVES):
                        dve.wait_ge(s_branch, 2 * CHUNKS * b + 2 * k + h + 1)
                        bank = p.use(job, h)[0]
                        ins = nc.vector.scalar_tensor_tensor(bank[:], bank[:], coef[:, h, 0:1], branch[h][:],
                                                             ALU.mult, ALU.max)
                    link(ins, b)
                    for h in range(HALVES):
                        at = X[q][:, h, tokens(k)]
                        nc.vector.scalar_tensor_tensor(at, p.use(job, h)[0][:], coef[:, h, 1:2], at,
                                                       ALU.add, ALU.add).then_inc(s_aux, 1)
                elif kind == "N2":
                    for i in range(2):
                        block_stats(p, job, i, b, q, 2 * k + i, BLOCKS // 2 + 2 * k + i)
                elif kind == "N2norm":
                    norm(b, q, k, EPS_T)
                elif kind == "TKkeys":
                    lg = logit[q]
                    dve.wait_ge(s_logit, CHUNKS * (b + 1))
                    nc.vector.tensor_tensor(tmp[0][:], rstd[:], small[:, LOGIT_COL:LOGIT_COL + BLOCKS], ALU.mult)
                    link(nc.vector.tensor_tensor(tmp[1][:], rstd[:], mean[:], ALU.mult), b)
                    link(nc.vector.scalar_tensor_tensor(tmp[2][:], tmp[1][:], rw_sum[:, 0:1], tmp[0][:],
                                                        ALU.mult, ALU.add), b)
                    link(nc.vector.tensor_scalar(lg[:], tmp[2][:], rb[:, 0:1], None, ALU.add), b)
                    bits = lg[:].bitcast(I32)
                    link(nc.vector.tensor_scalar(flip[:].bitcast(I32), bits, 31, -2 ** 31,
                                                 ALU.arith_shift_right, ALU.bitwise_or), b)
                    link(nc.vector.tensor_tensor(key[:].bitcast(I32), bits, flip[:].bitcast(I32), ALU.bitwise_xor), b)
                    nc.vector.tensor_scalar(key_hi[:], key[:], 16, None, ALU.logical_shift_right)
                    link(nc.vector.tensor_scalar(key_lo[:], key[:], 0xFFFF, None, ALU.bitwise_and), b)
                    nc.vector.memset(base[0][:], 0.0)
                    link(nc.vector.tensor_copy(digit_key[:], key_hi[:]), b)
                elif kind == "TK":
                    if k % 4:
                        digit_found(b, k - 1)
                    src = digit_key if k < 4 else low_key
                    link(nc.vector.tensor_scalar(tried[:], digits[:], 16.0 ** (3 - k % 4), base[k % 2][:, 0:1],
                                                 ALU.mult, ALU.add), b)
                    link(nc.vector.tensor_tensor(
                        above[:], src[:].unsqueeze(1).to_broadcast([P, DIGITS, BLOCKS]),
                        tried[:].unsqueeze(2).to_broadcast([P, DIGITS, BLOCKS]), ALU.is_ge), b)
                    with nc.allow_low_precision("counts up to 32 are exact in bfloat16"):
                        nc.vector.tensor_reduce(count[:], above[:], AX_X, ALU.add).then_inc(s_cnt, 1)
                elif kind == "TKlow":
                    digit_found(b, 3)
                    nc.vector.tensor_scalar(tmp[1][:], digit_key[:], base[0][:, 0:1], 70000.0, ALU.is_gt, ALU.mult)
                    link(nc.vector.tensor_scalar(tmp[0][:], digit_key[:], base[0][:, 0:1], None, ALU.is_equal), b)
                    link(nc.vector.scalar_tensor_tensor(tmp[2][:], key_lo[:], 1.0, tmp[0][:], ALU.add, ALU.mult), b)
                    nc.vector.tensor_tensor(low_key[:], tmp[2][:], tmp[1][:], ALU.add)
                    link(nc.vector.memset(base[0][:], 1.0), b)
                elif kind == "RANK":
                    digit_found(b, ROUNDS - 1)
                    nc.vector.tensor_scalar(gt_eq[:, 0, :], low_key[:], base[0][:, 0:1], None, ALU.is_gt)
                    nc.vector.tensor_scalar(gt_eq[:, 1, :], low_key[:], base[0][:, 0:1], None,
                                            ALU.is_equal).then_inc(s_cnt, 1)
                    dve.wait_ge(s_tot, (ROUNDS + 1) * (b + 1))
                    for i in range(2):
                        n = RANK_COL + (2 + i) * BLOCKS
                        ins = nc.vector.tensor_tensor_scan(incl[i][:], ones_row[:], small[:, n:n + BLOCKS], 0.0,
                                                           ALU.mult, ALU.add)
                    link(ins, b)
                    nc.vector.tensor_scalar(need[:], incl[0][:, BLOCKS - 1:BLOCKS], -1.0, float(CHOSEN),
                                            ALU.mult, ALU.add)
                    for i in range(2):
                        n = RANK_COL + (2 + i) * BLOCKS
                        ins = nc.vector.tensor_tensor(tmp[i][:], incl[i][:], small[:, n:n + BLOCKS], ALU.subtract)
                    link(ins, b)
                    for i in range(2):
                        n = RANK_COL + i * BLOCKS
                        ins = nc.vector.tensor_tensor(before[i][:], tmp[i][:], small[:, n:n + BLOCKS], ALU.add)
                    link(ins, b)
                    nc.vector.scalar_tensor_tensor(tmp[0][:], before[1][:], need[:, 0:1], gt_eq[:, 1, :],
                                                   ALU.is_lt, ALU.mult)
                    link(nc.vector.scalar_tensor_tensor(tmp[1][:], before[1][:], need[:, 0:1], before[0][:],
                                                        ALU.min, ALU.add), b)
                    link(nc.vector.tensor_tensor(chosen[:], tmp[0][:], gt_eq[:, 0, :], ALU.add), b)
                    nc.vector.tensor_tensor(logit[q][:], logit[q][:], chosen[:], ALU.mult)
                    link(nc.vector.tensor_scalar(tmp[2][:], chosen[:], -float(TOKENS), float(TOKENS),
                                                 ALU.mult, ALU.add), b)
                    nc.vector.tensor_tensor(index[q][:], tmp[2][:], tmp[1][:], ALU.add).then_inc(s_index, 1)
                elif kind == "FN":
                    for h in range(HALVES):
                        dve.wait_ge(s_fn, 2 * CHUNKS * b + 2 * k + h + 1)
                        at = X[q][:, h, tokens(k)]
                        nc.vector.tensor_tensor(at, p.use(job, h)[0][:], at, ALU.add).then_inc(s_aux, 1)

            def copy_y(b, q, f):
                dve.wait_ge(s_mm2, FCHUNKS * b + f + 1)
                if type(b) is not int or FCHUNKS * b + f > 0:
                    dve.wait_ge(s_ytab[(f - 1) % FCHUNKS], DMA * (b + (1 if f else 0)))
                for i in range(2):
                    ins = nc.vector.tensor_tensor(
                        y_rows[:, 2 * i:2 * i + 2, :], y_ps[i][:].rearrange("p (j c) -> p j c", j=2),
                        fb2[:].unsqueeze(1).to_broadcast([P, 2, C]), ALU.add)
                ins.then_inc(s_y, 1)

            def period(p):
                if p.ahead:
                    links[0] = 0
                for s in range(STEPS):
                    if p.ffn and s % HB == 0:
                        for h in range(HALVES):
                            dve.wait_ge(s_xshi, 2 * FCHUNKS * p.b + 2 * (s // HB) + h + 1)
                            nc.vector.tensor_tensor(xs_lo[:, h, :], p.use(("XS", 0, s // HB), h)[0][:],
                                                    xs_hi[:, h, :].bitcast(F32), ALU.subtract).then_inc(s_aux, 1)
                    for job in p.jobs(s):
                        stage(p, job)
                    if p.ffn:
                        dve.wait_ge(s_g, STEPS * p.b + s + 1)
                        r = s % G_RING
                        nc.vector.tensor_tensor(g_lo[r][:], h_ps[s % 2][:], g_hi[r][:].bitcast(F32),
                                                ALU.subtract).then_inc(s_glo, 1)
                    if s % HB == 1 and s > HB and p.ffn:
                        copy_y(p.b, p.q, s // HB - 1)
                    if s == 1 and p.prev:
                        copy_y(*p.image(-1), FCHUNKS - 1)
                if p.ahead:
                    CHAIN["image"] = links[0]

            run(dve, period)


def kernel(x, L0_conv_w1, L0_conv_b1, L0_conv_w2, L0_conv_b2, L0_ffn_attention_mask, L0_ffn_wr, L0_ffn_br,
           L0_ffn_w1, L0_ffn_b1, L0_ffn_w2, L0_ffn_b2):
    import concourse.bacc as bacc
    import numpy as np
    from concourse.bass_utils import run_bass_kernel_spmd

    images, channels, height, width = x.shape
    relu_h = L0_conv_w1.shape[0]
    groups = P // relu_h
    a = {k: np.asarray(v) for k, v in (
        ("w1", L0_conv_w1), ("b1", L0_conv_b1), ("w2", L0_conv_w2), ("b2", L0_conv_b2), ("wr", L0_ffn_wr),
        ("br", L0_ffn_br), ("f1", L0_ffn_w1), ("fb1", L0_ffn_b1), ("f2", L0_ffn_w2), ("fb2", L0_ffn_b2))}
    digits = 15
    consts = np.zeros((P, 2 * P + digits + groups), np.float32)
    consts[:, 0:P] = np.eye(P)
    consts[:, P:2 * P] = np.triu(np.ones((P, P)), 1)
    consts[:, 2 * P:2 * P + digits] = np.arange(1, digits + 1)
    consts[:, 2 * P + digits:] = np.kron(np.eye(groups), np.ones((relu_h, 1)))
    arrays = {
        "x": np.asarray(x).reshape(images, channels, height * width),
        "conv_w1": np.tile(a["w1"].T, (1, groups)),
        "conv_b1": np.tile(a["b1"], groups)[:, None],
        "conv_w2": a["w2"].reshape(2, channels, 2, relu_h).transpose(0, 2, 3, 1).reshape(P, channels),
        "conv_b2": a["b2"].reshape(2, channels // P, P, 2).transpose(2, 1, 0, 3).reshape(P, -1, groups),
        "router_w": a["wr"].reshape(-1, P).T,
        "router_b": np.tile(a["br"], P)[:, None],
        "ffn_w1": a["f1"],
        "ffn_b1": a["fb1"].reshape(-1, P).T,
        "ffn_w2": a["f2"],
        "ffn_b2": np.tile(a["fb2"], (P, 1)),
        "consts": consts,
    }
    arrays = {k: np.ascontiguousarray(v) for k, v in arrays.items()}
    from concourse import mybir as _mybir

    nc = bacc.Bacc("TRN2", target_bir_lowering=False, num_devices=1, dynamic_dma_scratch_size=8192)
    args = {k: nc.dram_tensor(k, v.shape, _mybir.dt.from_np(v.dtype), kind="ExternalInput").ap()
            for k, v in arrays.items()}
    out = nc.dram_tensor("out", arrays["x"].shape, F32, kind="ExternalOutput").ap()
    metaformer_kernel(nc, out=out, **args)
    r = run_bass_kernel_spmd(nc, [arrays], core_ids=[0])
    return r.results[0]["out"].reshape(images, channels, height, width)
```

```python
from contextlib import ExitStack

from concourse import mybir
from concourse.bass import IndirectOffsetOnAxis

ALU = mybir.AluOpType
ACT = mybir.ActivationFunctionType
F32 = mybir.dt.float32
F32R = mybir.dt.float32r
BF16 = mybir.dt.bfloat16
I32 = mybir.dt.int32
U32 = mybir.dt.uint32
AX_X = mybir.AxisListType.X

P = 128
DMA = 16
LAG = 2
G_RING = 3
AUX = 3
TURN = 3
OUT_RING = 4
EPS_C = 1e-6
EPS_T = 1e-5


AT = dict(CV=-1.0, CVd=1.5, N2=0.5, N2d=1.5, N2M=12.0, TK=13.0, TKd=0.75, RANK=20.0, SC=21.0,
          FN=4.5, FNd=2.1, N1=5.5, N1d=2.1, N1M=22.5, NORM=23.0, NORMd=0.5, SE=28.0)


def plan(chunks, steps):
    slots = {e: [[] for _ in range(2 * steps)] for e in ("SP", "POOL", "PE", "ACT", "DVE")}

    def put(stage, off, k, **at):
        for engine, step in at.items():
            periods, slot = divmod(int(round(2 * step)), 2 * steps)
            slots[engine][slot].append((stage, off - periods, k))

    for k in range(chunks):
        t = AT["CV"] + AT["CVd"] * k
        put("CV", 1, k, PE=t, ACT=t, DVE=t + 0.5)
    for k in range(chunks):
        t = AT["N2"] + AT["N2d"] * k
        put("N2", 1, k, PE=t, ACT=t, DVE=t + 0.5)
        put("LOAD", 2, k, SP=t)
    put("N2M", 1, 0, DVE=AT["N2M"])
    for r in range(8):
        t = AT["TK"] + AT["TKd"] * r
        put("TK", 1, r, DVE=t, PE=t + 0.5)
    put("RANK1", 1, 0, DVE=AT["RANK"], PE=AT["RANK"] + 0.5)
    put("RANK2", 1, 0, DVE=AT["RANK"] + 1)
    put("SC", 1, 0, POOL=AT["SC"])
    for c in range(chunks):
        t = AT["FN"] + AT["FNd"] * c
        put("FN", -1, c, POOL=t - 2, DVE=t - 0.5, PE=t, ACT=t, SP=t)
    for g in range(2 * chunks):
        t = AT["N1"] + AT["N1d"] * (g // 2) + 0.5 * (g % 2)
        put("N1", 2, g, PE=t, ACT=t, DVE=t + 0.5)
    put("N1M", 2, 0, DVE=AT["N1M"])
    for k in range(chunks):
        t = AT["NORM"] + AT["NORMd"] * k
        put("NORM", 2, k, ACT=t, PE=t + 0.5)
    t = AT["SE"]
    put("SE1", 2, 0, DVE=t, PE=t + 0.5, ACT=t + 0.5)
    put("SE2", 2, 0, DVE=t + 1, PE=t + 1.5)
    put("SE3", 2, 0, DVE=t + 2, ACT=t + 2)
    put("SE4", 2, 0, DVE=t + 2.5)
    return slots


def bank_uses(plan_, steps, steps_of_chunk, offsets):
    uses = []
    for s in range(steps):
        if 0 in offsets and s % steps_of_chunk == 0:
            uses += [("XS", 0, s // steps_of_chunk, h) for h in range(2)]
        for job in plan_["PE"][2 * s] + plan_["PE"][2 * s + 1]:
            if job[1] in offsets:
                uses += [job + (h,) for h in range({"N1": 1, "N2": 2, "CV": 2, "FN": 2}.get(job[0], 0))]
    return uses


def metaformer_kernel(nc, x, conv_w1, conv_b1, conv_w2, conv_b2, router_w, router_b, ffn_w1, ffn_b1,
                      ffn_w2, ffn_b2, consts, out):
    IMAGES, C, TOKENS = x.shape
    H = ffn_w1.shape[1]
    HALVES = C // P
    BLOCKS = TOKENS // P
    CHUNK = 512
    CHUNKS = TOKENS // CHUNK
    SLOTS = TOKENS // 2
    CHOSEN = SLOTS - 1
    FCHUNKS = SLOTS // CHUNK
    HB = H // P
    STEPS = FCHUNKS * HB
    KGROUPS = 4
    RELU_H = P // KGROUPS
    DIGITS = 15
    ROUNDS = 8
    assert IMAGES > 2 * TURN
    ROW = C + 2
    PLAN = plan(CHUNKS, STEPS)

    xT = x.rearrange("b (h p) t -> b p h t", p=P)
    oT = out.rearrange("b (h p) t -> b p h t", p=P)

    ctx = ExitStack()
    with ctx:
        def sb(name, shape, dt):
            return ctx.enter_context(nc.sbuf_tensor(name, shape, dt))

        def sem(name):
            return ctx.enter_context(nc.semaphore(name))

        X = sb("X", [P, HALVES, TOKENS], F32)
        T = [sb(f"T{q}", [P, BLOCKS, ROW], F32) for q in range(TURN)]
        out_sb = [sb(f"out_sb{r}", [P, CHUNK], F32) for r in range(OUT_RING)]
        w1_hi = sb("w1_hi", [P, HALVES, H], F32R)
        w1_lo = sb("w1_lo", [P, HALVES, H], F32R)
        w2_hi = sb("w2_hi", [P, HB, C], F32R)
        w2_lo = sb("w2_lo", [P, HB, C], F32R)
        g_hi = [sb(f"g_hi{r}", [P, CHUNK], F32R) for r in range(G_RING)]
        g_lo = [sb(f"g_lo{r}", [P, CHUNK], F32R) for r in range(G_RING)]
        rows = sb("rows", [P, 4, ROW], F32)
        xs_hi = sb("xs_hi", [P, HALVES, CHUNK], F32R)
        xs_lo = sb("xs_lo", [P, HALVES, CHUNK], F32R)
        y_rows = sb("y_rows", [P, 4, C], F32)
        y_back = sb("y_back", [P, 8, C], F32)
        branch = [sb(f"branch{r}", [P, CHUNK], F32) for r in range(2)]
        ident = sb("ident", [P, P], F32)
        tri = sb("tri", [P, P], BF16)
        digits = sb("digits", [P, DIGITS], F32)
        ones_f = sb("ones_f", [P, 1], F32)
        ones_b = sb("ones_b", [P, P], BF16)
        cw1 = sb("cw1", [P, HALVES, P], F32)
        cb1 = sb("cb1", [P, 1], F32)
        cw2 = sb("cw2", [P, C], F32)
        cb2 = sb("cb2", [P, HALVES, KGROUPS], F32)
        rw = sb("rw", [P, HALVES], F32)
        rb = sb("rb", [P, 1], F32)
        rw_sum = sb("rw_sum", [P, 1], F32)
        fb1 = sb("fb1", [P, HB], F32)
        fb2 = sb("fb2", [P, C], F32)
        stats = [sb(f"stats{n}", [P, BLOCKS, 6], F32) for n in range(2)]
        tmp = [sb(f"tmp{i}", [P, BLOCKS], F32) for i in range(4)]
        offset1 = sb("offset1", [P, BLOCKS], F32)
        mean = [sb(f"mean{n}", [P, BLOCKS], F32) for n in range(2)]
        rstd = [sb(f"rstd{n}", [P, BLOCKS], F32) for n in range(2)]
        z_scale = sb("z_scale", [P, BLOCKS], F32)
        z_offset = sb("z_offset", [P, BLOCKS], F32)
        pooled = sb("pooled", [P, HALVES], F32)
        hid = sb("hid", [P, 1], F32)
        group_mask = sb("group_mask", [P, KGROUPS], F32)
        hid4 = sb("hid4", [P, KGROUPS], F32)
        pre = sb("pre", [P, HALVES, KGROUPS], F32)
        delta = sb("delta", [P, HALVES, KGROUPS], F32)
        coef = sb("coef", [P, HALVES, KGROUPS], F32)
        logit = [sb(f"logit{q}", [P, BLOCKS], F32) for q in range(TURN)]
        index = [sb(f"index{q}", [P, BLOCKS], U32) for q in range(TURN)]
        flip = sb("flip", [P, BLOCKS], U32)
        key = sb("key", [P, BLOCKS], U32)
        key_hi = sb("key_hi", [P, BLOCKS], U32)
        key_lo = sb("key_lo", [P, BLOCKS], U32)
        digit_key = sb("digit_key", [P, BLOCKS], F32)
        low_key = sb("low_key", [P, BLOCKS], F32)
        base = [sb(f"base{i}", [P, 1], F32) for i in range(2)]
        tried = sb("tried", [P, DIGITS], F32)
        above = sb("above", [P, DIGITS, BLOCKS], BF16)
        count = sb("count", [P, DIGITS], BF16)
        junk = sb("junk", [P, DIGITS], F32)
        passed = sb("passed", [P, 1], F32)
        gt_eq = sb("gt_eq", [P, 2, BLOCKS], BF16)
        incl = [sb(f"incl{i}", [P, BLOCKS], F32) for i in range(2)]
        before = [sb(f"before{i}", [P, BLOCKS], F32) for i in range(2)]
        need = sb("need", [P, 1], F32)
        chosen = sb("chosen", [P, BLOCKS], F32)
        ones_row = sb("ones_row", [P, BLOCKS], F32)

        psum = [ctx.enter_context(nc.psum_tensor(f"psum{i}", [P, 512], F32)) for i in range(8)]
        y_ps, h_ps, aux_ps, small = psum[0:2], psum[2:4], psum[4:4 + AUX], psum[7]
        POOL_COL, LOGIT_COL, SE_COL, CNT_COL, RANK_COL = 0, 64, 96, 112, 128
        RWS_COL = 300
        x_table = [nc.dram_tensor(f"x_table{q}", (SLOTS, ROW), F32).ap() for q in range(TURN)]
        y_table = [nc.dram_tensor(f"y_table{q}", (SLOTS, C), F32).ap() for q in range(TURN)]

        s_const = sem("s_const")
        s_met = sem("s_met")
        s_wload = sem("s_wload")
        s_zero = sem("s_zero")
        s_zrow = sem("s_zrow")
        s_wsplit = sem("s_wsplit")
        s_rws = sem("s_rws")
        s_xin = [sem(f"s_xin{k}") for k in range(CHUNKS)]
        s_out = [sem(f"s_out{r}") for r in range(OUT_RING)]
        s_tok = [sem(f"s_tok{n}") for n in range(2)]
        s_copied = [sem(f"s_copied{n}") for n in range(2)]
        s_mom = sem("s_mom")
        s_norm = sem("s_norm")
        s_pool = sem("s_pool")
        s_pooled = sem("s_pooled")
        s_hid = sem("s_hid")
        s_hidr = sem("s_hidr")
        s_se = sem("s_se")
        s_pre = sem("s_pre")
        s_delta = sem("s_delta")
        s_coef = sem("s_coef")
        s_cv = sem("s_cv")
        s_branch = sem("s_branch")
        s_logit = sem("s_logit")
        s_cnt = sem("s_cnt")
        s_tot = sem("s_tot")
        s_index = sem("s_index")
        s_scat = sem("s_scat")
        s_rows = sem("s_rows")
        s_cn = sem("s_cn")
        s_xs = sem("s_xs")
        s_xshi = sem("s_xshi")
        s_h = sem("s_h")
        s_g = sem("s_g")
        s_glo = sem("s_glo")
        s_mm2 = sem("s_mm2")
        s_y = sem("s_y")
        s_ytab = [sem(f"s_ytab{f}") for f in range(FCHUNKS)]
        s_back = [sem(f"s_back{i}") for i in range(2)]
        s_added = sem("s_added")
        s_fn = sem("s_fn")
        s_hid4 = sem("s_hid4")
        s_x2 = sem("s_x2")
        s_outc = sem("s_outc")
        s_xslo = sem("s_xslo")
        s_chain = sem("s_chain")


        block = ctx.enter_context(nc.Block())
        FULL = (-1, 0, 1, 2)
        FIRST_FULL, N_FULL = 1, IMAGES - TURN

        class Period:

            def __init__(self, b, q, offsets, before, used):
                self.b, self.q, self.offsets = b, q, offsets
                self.full = offsets == FULL
                self.uses = bank_uses(PLAN, STEPS, HB, offsets)
                self.before = before
                self.used = used

            def image(self, off):
                return self.b + off, (self.q + off) % TURN

            def jobs(self, engine, slot):
                return [job for job in PLAN[engine][slot] if job[1] in self.offsets]

            def tail(self):
                return [(kind, off - 1, k, h) for kind, off, k, h in (self.before + self.uses)[-AUX:]]

            def bank(self, job, h=0):
                return aux_ps[(self.used + self.uses.index(job + (h,))) % AUX]

            def bank_before(self, use):
                n = self.uses.index(use)
                return (self.before + self.uses)[n] if len(self.before) == AUX else (
                    self.uses[n - AUX] if n >= AUX else None)

        def run(eng, period):
            used, tail = 0, []
            for b, offsets in ((-2, (2,)), (-1, (1, 2)), (0, (0, 1, 2))):
                p = Period(b, b % TURN, offsets, tail, used)
                period(p)
                used, tail = used + len(p.uses), p.tail()
            full = Period(None, 0, FULL, tail, used)
            assert full.tail() == tail and len(full.uses) % AUX == 0
            peeled = (N_FULL - 1) % TURN + 1
            for b in range(FIRST_FULL, FIRST_FULL + peeled):
                period(Period(b, b % TURN, FULL, tail, used))
            b0 = FIRST_FULL + peeled
            with eng.Fori(0, (N_FULL - peeled) // TURN) as i:
                for k in range(TURN):
                    b = nc.snap(i * TURN + (b0 + k), engines=[eng.engine], min_val=b0 + k, max_val=IMAGES - TURN)
                    period(Period(b, (b0 + k) % TURN, FULL, tail, used))
            for b, offsets in ((IMAGES - 2, (-1, 0, 1)), (IMAGES - 1, (-1, 0)), (IMAGES, (-1,))):
                p = Period(b, b % TURN, offsets, tail, used)
                period(p)
                used, tail = used + len(p.uses), p.tail()

        def settled(eng):
            eng.sem_inc(s_met, 1)

        def tokens(k, n=CHUNK):
            return slice(k * n, (k + 1) * n)

        def g_place(q, s):
            return (q * STEPS + s) % G_RING

        stage_area = T[1][:].rearrange("p j c -> p (j c)")
        w1_raw = stage_area[:, 0:HALVES * H].rearrange("p (h m) -> p h m", h=HALVES)
        w2_raw = stage_area[:, HALVES * H:HALVES * H + HB * C].rearrange("p (h c) -> p h c", h=HB)
        ones_sq = stage_area[:, 6 * H:6 * H + P]
        tri_f = stage_area[:, 6 * H + P:6 * H + 2 * P]

        @block.sync
        def _(sp):
            for dst, src in ((ident[:], consts[:, 0:P]), (tri_f, consts[:, P:2 * P]),
                             (digits[:], consts[:, 2 * P:2 * P + DIGITS]),
                             (group_mask[:], consts[:, 2 * P + DIGITS:2 * P + DIGITS + KGROUPS]),
                             (cw1[:], conv_w1.rearrange("(h p) m -> p h m", p=P)), (cb1[:], conv_b1),
                             (cw2[:], conv_w2), (cb2[:], conv_b2), (rw[:], router_w), (rb[:], router_b),
                             (fb1[:], ffn_b1), (fb2[:], ffn_b2)):
                sp.dma_start(dst, src).then_inc(s_const, DMA)
            sp.dma_start(w1_raw, ffn_w1.rearrange("(h p) m -> p h m", p=P)).then_inc(s_wload, DMA)
            sp.dma_start(w2_raw, ffn_w2.rearrange("(h p) m -> p h m", p=P)).then_inc(s_wload, DMA)
            sp.wait_ge(s_zero, 2)
            for q in range(TURN):
                sp.dma_start(x_table[q][SLOTS - 1:SLOTS, 0:C], y_back[0:1, 0, :]).then_inc(s_zrow, DMA)
                sp.dma_start(x_table[q][SLOTS - 1:SLOTS, C:ROW], y_back[0:1, 1, 0:2]).then_inc(s_zrow, DMA)
            sp.wait_ge(s_zrow, 2 * TURN * DMA)

            def period(p):
                for s in range(STEPS):
                    if s % HB == 1 and (0 if s > HB else -1) in p.offsets:
                        b, q = p.image(0 if s > HB else -1)
                        f = (s // HB - 1) % FCHUNKS
                        sp.wait_ge(s_y, FCHUNKS * b + f + 1)
                        settled(sp)
                        sp.dma_start(y_table[q][f * CHUNK:(f + 1) * CHUNK, :].rearrange("(p i) c -> p i c", i=4),
                                     y_rows[:]).then_inc(s_ytab[f], DMA)
                    for kind, off, k in p.jobs("SP", 2 * s) + p.jobs("SP", 2 * s + 1):
                        b, q = p.image(off)
                        if kind == "LOAD":
                            if type(b) is not int or b > 0:
                                sp.wait_ge(s_logit, CHUNKS * (b - 1) + k + 1)
                                settled(sp)
                            sp.dma_start(X[:, :, tokens(k)], xT[b, :, :, tokens(k)]).then_inc(s_xin[k], DMA)
                        elif kind == "FN":
                            for h in range(HALVES):
                                r = HALVES * (k % 2) + h
                                sp.wait_ge(s_outc, HALVES * CHUNKS * b + HALVES * k + h + 1)
                                settled(sp)
                                sp.dma_start(oT[b, :, h, tokens(k)], out_sb[r][:]).then_inc(s_out[r], DMA)
                if 1 in p.offsets:
                    b, q = p.image(1)
                    if 0 in p.offsets:
                        sp.wait_ge(s_xs, 2 * FCHUNKS * b)
                        settled(sp)
                    sp.wait_ge(s_scat, DMA * BLOCKS * (b + 1))
                    settled(sp)
                    sp.dma_start(rows[:], x_table[q][0:CHUNK, :].rearrange("(p i) c -> p i c", i=4)
                                 ).then_inc(s_rows, DMA)

            run(sp, period)
            for r in range(OUT_RING):
                sp.wait_ge(s_out[r], DMA * HALVES * CHUNKS // OUT_RING * IMAGES)

        @block.gpsimd
        def _(pool):
            nc.gpsimd.memset(y_back[:], 0.0).then_inc(s_zero, 1)

            def period(p):
                for slot in range(2 * STEPS):
                    for kind, off, k in p.jobs("POOL", slot):
                        b, q = p.image(off)
                        if kind == "FN":
                            known = min(CHUNK * (k + 1), SLOTS)
                            pool.wait_ge(s_ytab[min(k, FCHUNKS - 1)], DMA * (b + 1))
                            settled(pool)
                            if type(b) is not int or CHUNKS * b + k - 1 > 0:
                                pool.wait_ge(s_added, CHUNKS * b + k - 1)
                                settled(pool)
                            for i in range(4):
                                j = 4 * k + i
                                pool.indirect_dma_start(
                                    y_back[:, 4 * (k % 2) + i, :], None, y_table[q][0:known, :],
                                    IndirectOffsetOnAxis(ap=index[q][:, j:j + 1], axis=0),
                                    bounds_check=min(known, CHOSEN) - 1, oob_is_err=False).then_inc(s_back[k % 2], DMA)
                        elif kind == "SC":
                            pool.wait_ge(s_index, b + 1)
                            settled(pool)
                            for j in range(BLOCKS):
                                pool.indirect_dma_start(
                                    x_table[q], IndirectOffsetOnAxis(ap=index[q][:, j:j + 1], axis=0),
                                    T[q][:, j, :], None,
                                    bounds_check=CHOSEN - 1, oob_is_err=False).then_inc(s_scat, DMA)

            run(pool, period)

        @block.tensor
        def _(pe):
            pe.wait_ge(s_const, DMA * 12)
            pe.wait_ge(s_wsplit, 1)
            for h in range(HALVES):
                rws = nc.tensor.matmul(small[:, RWS_COL:RWS_COL + 1], ones_sq, rw[:, h:h + 1],
                                       start=(h == 0), stop=(h == HALVES - 1))
            rws.then_inc(s_rws, 1)

            def flip_block(out, src, **flags):
                return nc.tensor.matmul(out, src, ident[:], is_transpose=True, skip_group_check=True, **flags)

            def bank_of(p, job, h=0):
                last = p.bank_before(job + (h,))
                if last is not None:
                    kind, off, k, i = last
                    b = p.b + off
                    if kind in ("N1", "N2"):
                        n = 2 * CHUNKS * b + (k if kind == "N1" else 2 * k + i) + 1
                        pe.wait_ge(s_copied[0 if kind == "N1" else 1], n)
                    elif kind == "CV":
                        pe.wait_ge(s_x2, 2 * CHUNKS * b + 2 * k + i + 1)
                    elif kind == "FN":
                        pe.wait_ge(s_outc, 2 * CHUNKS * b + 2 * k + i + 1)
                    else:
                        pe.wait_ge(s_xslo, 2 * FCHUNKS * b + 2 * k + i + 1)
                return p.bank(job, h)

            def to_tokens(p, job, h, done, pair):
                bank = bank_of(p, job, h)
                for i in range(2):
                    for half in range(HALVES):
                        t = flip_block(bank[:, i * C + half * P:i * C + (half + 1) * P],
                                       X[:, half, tokens(2 * pair + i, P)], start=(i + half == 0), stop=True)
                t.then_inc(done, 1)

            def to_channels(p, job, h, done):
                b, q = p.image(job[1])
                bank = bank_of(p, job, h)
                for i in range(4):
                    t = flip_block(bank[:, tokens(i, P)], T[q][:, 4 * job[2] + i, h * P:(h + 1) * P],
                                   start=(i == 0), stop=True)
                t.then_inc(done, 1)

            def stage(p, job):
                kind, off, k = job
                b, q = p.image(off)
                if kind == "N1":
                    if k % 2 == 0:
                        pe.wait_ge(s_xin[k // 2], DMA * (b + 1))
                    to_tokens(p, job, 0, s_tok[0], k)
                elif kind == "NORM":
                    pe.wait_ge(s_norm, CHUNKS * b + k + 1)
                    for j in range(4 * k, 4 * k + 4):
                        for h in range(HALVES):
                            col = POOL_COL + h * BLOCKS + j
                            m = nc.tensor.matmul(small[:, col:col + 1], T[q][:, j, h * P:(h + 1) * P],
                                                 ones_f[:, 0:1], start=True, stop=True)
                    if k == CHUNKS - 1:
                        m.then_inc(s_pool, 1)
                elif kind == "SE1":
                    pe.wait_ge(s_pooled, b + 1)
                    for h in range(HALVES):
                        m = nc.tensor.matmul(small[:, SE_COL:SE_COL + 1], cw1[:, h, :], pooled[:, h:h + 1],
                                             start=(h == 0), stop=(h == HALVES - 1))
                    m.then_inc(s_hid, 1)
                elif kind == "SE2":
                    pe.wait_ge(s_hid4, b + 1)
                    for h in range(HALVES):
                        col = SE_COL + 1 + KGROUPS * h
                        m = nc.tensor.matmul(small[:, col:col + KGROUPS], cw2[:, h * P:(h + 1) * P], hid4[:],
                                             start=True, stop=True)
                    m.then_inc(s_se, 1)
                elif kind == "CV":
                    for h in range(HALVES):
                        to_channels(p, job, h, s_cv)
                elif kind == "N2":
                    pe.wait_ge(s_x2, 2 * CHUNKS * b + 2 * k + 2)
                    for i in range(2):
                        to_tokens(p, job, i, s_tok[1], 2 * k + i)
                    for j in range(4 * k, 4 * k + 4):
                        for h in range(HALVES):
                            m = nc.tensor.matmul(small[:, LOGIT_COL + j:LOGIT_COL + j + 1],
                                                 X[:, h, tokens(j, P)], rw[:, h:h + 1],
                                                 start=(h == 0), stop=(h == HALVES - 1))
                    m.then_inc(s_logit, 1)
                elif kind == "TK":
                    pe.wait_ge(s_cnt, (ROUNDS + 1) * b + k + 1)
                    nc.tensor.matmul(small[:, CNT_COL:CNT_COL + DIGITS], ones_b[:], count[:],
                                     start=True, stop=True).then_inc(s_tot, 1)
                elif kind == "RANK1":
                    pe.wait_ge(s_cnt, (ROUNDS + 1) * (b + 1))
                    both = gt_eq[:].rearrange("p a j -> p (a j)")
                    nc.tensor.matmul(small[:, RANK_COL:RANK_COL + 2 * BLOCKS], tri[:], both,
                                     start=True, stop=True)
                    nc.tensor.matmul(small[:, RANK_COL + 2 * BLOCKS:RANK_COL + 4 * BLOCKS], ones_b[:], both,
                                     start=True, stop=True).then_inc(s_tot, 1)
                elif kind == "FN":
                    pe.wait_ge(s_added, CHUNKS * b + k + 1)
                    for h in range(HALVES):
                        to_channels(p, job, h, s_fn)

            def first_product(p, s):
                h, bank = s % HB, h_ps[s % 2]
                if s % HB == 0:
                    pe.wait_ge(s_xslo, 2 * FCHUNKS * p.b + 2 * (s // HB) + 2)
                if s >= 2 or -1 in p.offsets:
                    pe.wait_ge(s_glo, STEPS * p.b + s - 1)
                n = 0
                for half in range(HALVES):
                    for w, v in ((w1_hi, xs_hi), (w1_lo, xs_hi), (w1_hi, xs_lo)):
                        m = nc.tensor.matmul(bank[:], w[:, half, h * P:(h + 1) * P], v[:, half, :],
                                             start=(n == 0), stop=(n == 5))
                        n += 1
                m.then_inc(s_h, 1)

            def second_product(b, q, s):
                h, f, r = s % HB, s // HB, g_place(q, s)
                pe.wait_ge(s_glo, STEPS * b + s + 1)
                if h == 0 and (type(b) is not int or FCHUNKS * b + f > 0):
                    pe.wait_ge(s_y, FCHUNKS * b + f)
                for i in range(4):
                    for n, (g, w) in enumerate(((g_hi, w2_hi), (g_lo, w2_hi), (g_hi, w2_lo))):
                        m = nc.tensor.matmul(y_ps[i // 2][:, (i % 2) * C:(i % 2 + 1) * C],
                                             g[r][:, tokens(i, P)], w[:, h, :],
                                             start=(h == 0 and n == 0 and i % 2 == 0),
                                             stop=(h == HB - 1 and n == 2), skip_group_check=True)
                if h == HB - 1:
                    m.then_inc(s_mm2, 1)

            def period(p):
                ffn = 0 in p.offsets
                for s in range(STEPS):
                    if ffn and s % HB == 0:
                        f = s // HB
                        pe.wait_ge(s_cn, FCHUNKS * p.b + f + 1)
                        for h in range(HALVES):
                            bank = bank_of(p, ("XS", 0, f), h)
                            for i in range(4):
                                t = flip_block(bank[:, tokens(i, P)], rows[:, i, h * P:(h + 1) * P],
                                               start=(i == 0), stop=True)
                            t.then_inc(s_xs, 1)
                    if ffn:
                        first_product(p, s)
                    for job in p.jobs("PE", 2 * s):
                        stage(p, job)
                    if s < LAG and -1 in p.offsets:
                        second_product(*p.image(-1), STEPS + s - LAG)
                    if s >= LAG and ffn:
                        second_product(*p.image(0), s - LAG)
                    for job in p.jobs("PE", 2 * s + 1):
                        stage(p, job)

            run(pe, period)

        @block.scalar
        def _(act):
            def stage(p, job):
                kind, off, k = job
                b, q = p.image(off)
                if kind in ("N1", "N2"):
                    for i in range(1 if kind == "N1" else 2):
                        n = k if kind == "N1" else 2 * k + i
                        which = 0 if kind == "N1" else 1
                        act.wait_ge(s_tok[which], BLOCKS // 2 * b + n + 1)
                        nc.scalar.copy(T[q][:, 2 * n:2 * n + 2, 0:C],
                                       p.bank(job, i)[:].rearrange("p (j c) -> p j c", j=2)
                                       ).then_inc(s_copied[which], 1)
                elif kind == "NORM":
                    if k == 0:
                        act.wait_ge(s_mom, b + 1)
                    for j in range(4 * k, 4 * k + 4):
                        row = T[q][:, j, 0:C]
                        a = nc.scalar.activation(row, row, ACT.Identity, bias=offset1[:, j:j + 1],
                                                 scale=rstd[0][:, j:j + 1])
                    a.then_inc(s_norm, 1)
                elif kind == "SE1":
                    act.wait_ge(s_hid, b + 1)
                    nc.scalar.activation(hid[:], small[:, SE_COL:SE_COL + 1], ACT.Relu, bias=cb1[:, 0:1],
                                         scale=1.0 / TOKENS).then_inc(s_hidr, 1)
                elif kind == "SE3":
                    act.wait_ge(s_pre, b + 1)
                    nc.scalar.activation(delta[:], pre[:], ACT.Tanh, scale=0.5).then_inc(s_delta, 1)
                elif kind == "CV":
                    if k == 0:
                        act.wait_ge(s_coef, b + 1)
                    for h in range(HALVES):
                        act.wait_ge(s_cv, 2 * CHUNKS * b + 2 * k + h + 1)
                        if k:
                            act.wait_ge(s_x2, 2 * CHUNKS * b + 2 * k + h - 1)
                        nc.scalar.activation(branch[h][:], p.bank(job, h)[:], ACT.Identity,
                                             bias=coef[:, h, 3:4], scale=coef[:, h, 2:3]).then_inc(s_branch, 1)
                elif kind == "FN":
                    for h in range(HALVES):
                        r = HALVES * (k % 2) + h
                        act.wait_ge(s_fn, 2 * CHUNKS * b + 2 * k + h + 1)
                        if type(b) is not int or CHUNKS // 2 * b + k // 2 > 0:
                            act.wait_ge(s_out[r], DMA * (CHUNKS // 2 * b + k // 2))
                        nc.scalar.copy(out_sb[r][:], p.bank(job, h)[:]).then_inc(s_outc, 1)

            def norm_rows(p, f):
                act.wait_ge(s_rows, DMA * (FCHUNKS * p.b + f + 1))
                for i in range(4):
                    row = rows[:, i, 0:C]
                    a = nc.scalar.activation(row, row, ACT.Identity, bias=rows[:, i, C:C + 1],
                                             scale=rows[:, i, C + 1:C + 2])
                a.then_inc(s_cn, 1)

            def period(p):
                ffn = 0 in p.offsets
                if type(p.b) is int and p.b == -1:
                    act.wait_ge(s_wsplit, 2)
                if ffn:
                    norm_rows(p, 0)
                for s in range(STEPS):
                    if ffn and s % HB == 0:
                        f = s // HB
                        for h in range(HALVES):
                            act.wait_ge(s_xs, 2 * FCHUNKS * p.b + 2 * f + h + 1)
                            nc.scalar.copy(xs_hi[:, h, :], p.bank(("XS", 0, f), h)[:]).then_inc(s_xshi, 1)
                        if f + 1 < FCHUNKS:
                            act.dma_start(rows[:], x_table[p.q][(f + 1) * CHUNK:(f + 2) * CHUNK, :]
                                          .rearrange("(p i) c -> p i c", i=4)).then_inc(s_rows, DMA)
                    if ffn:
                        act.wait_ge(s_h, STEPS * p.b + s + 1)
                        bank, h = h_ps[s % 2], s % HB
                        nc.scalar.activation(g_hi[g_place(p.q, s)][:], bank[:], ACT.Gelu_apprx_tanh,
                                             bias=fb1[:, h:h + 1])
                        nc.scalar.activation(bank[:], bank[:], ACT.Gelu_apprx_tanh,
                                             bias=fb1[:, h:h + 1]).then_inc(s_g, 1)
                    for job in p.jobs("ACT", 2 * s):
                        stage(p, job)
                    if ffn and s % HB == HB - 3 and s // HB + 1 < FCHUNKS:
                        norm_rows(p, s // HB + 1)
                    for job in p.jobs("ACT", 2 * s + 1):
                        stage(p, job)

            act.wait_ge(s_const, DMA * 12)
            run(act, period)

        @block.vector
        def _(dve):
            chain = {"before": 0, "here": 0}

            def mark(ins):
                chain["here"] += 1
                ins.then_inc(s_chain, 1)
                return chain["before"] + chain["here"]

            def link(ins, *between):
                n = mark(ins)
                for other in between:
                    other()
                dve.wait_ge(s_chain, n)

            nc.vector.memset(ones_f[:], 1.0)
            nc.vector.memset(ones_sq, 1.0)
            nc.vector.memset(ones_row[:], 1.0)
            nc.vector.memset(ones_b[:], 1.0).then_inc(s_zero, 1)
            dve.wait_ge(s_const, DMA * 12)
            nc.vector.tensor_copy(tri[:], tri_f).then_inc(s_wsplit, 1)
            dve.wait_ge(s_rws, 1)
            link(nc.vector.tensor_scalar(rw_sum[:], small[:, RWS_COL:RWS_COL + 1], -1.0, None, ALU.mult))
            dve.wait_ge(s_wload, 2 * DMA)
            nc.vector.tensor_copy(w1_hi[:], w1_raw)
            link(nc.vector.tensor_copy(w2_hi[:], w2_raw))
            nc.vector.tensor_tensor(w1_lo[:], w1_raw, w1_hi[:].bitcast(F32), ALU.subtract)
            nc.vector.tensor_tensor(w2_lo[:], w2_raw, w2_hi[:].bitcast(F32), ALU.subtract).then_inc(s_wsplit, 1)

            def block_stats(n, b, q, pair):
                dve.wait_ge(s_copied[n], BLOCKS // 2 * b + pair + 1)
                for j in (2 * pair, 2 * pair + 1):
                    ins = nc.vector.bn_stats(stats[n][:, j, :], T[q][:, j, 0:C])
                if j == BLOCKS - 1:
                    stats_done[n] = mark(ins)

            stats_done = [0, 0]

            def moments(n, eps):
                a, d, v, u = (t[:] for t in tmp)
                m, r, st = mean[n][:], rstd[n][:], stats[n]
                dve.wait_ge(s_chain, stats_done[n])
                nc.vector.tensor_tensor(d, st[:, :, 1], st[:, :, 4], ALU.subtract)
                nc.vector.tensor_tensor(a, st[:, :, 1], st[:, :, 4], ALU.add)
                link(nc.vector.tensor_tensor(v, st[:, :, 2], st[:, :, 5], ALU.add))
                nc.vector.tensor_scalar(m, a, 0.5, None, ALU.mult)
                link(nc.vector.tensor_tensor(u, d, d, ALU.mult))
                link(nc.vector.scalar_tensor_tensor(a, u, C / 4.0, v, ALU.mult, ALU.add))
                link(nc.vector.tensor_scalar(v, a, 1.0 / C, eps, ALU.mult, ALU.add))
                link(nc.vector.tensor_scalar(r.bitcast(I32), v.bitcast(I32), -0.5, 1597463007.0, ALU.mult, ALU.add))
                for _ in range(3):
                    link(nc.vector.tensor_tensor(a, r, r, ALU.mult))
                    link(nc.vector.scalar_tensor_tensor(u, a, -0.5, v, ALU.mult, ALU.mult))
                    link(nc.vector.scalar_tensor_tensor(r, u, 1.5, r, ALU.add, ALU.mult))

            def z_row(q, j):
                def run_it():
                    row = T[q][:, j, 0:C]
                    nc.vector.tensor_scalar(row, row, z_scale[:, j:j + 1], z_offset[:, j:j + 1],
                                            ALU.mult, ALU.add)
                return run_it

            def digit_found(b, k, first, second):
                dve.wait_ge(s_tot, (ROUNDS + 1) * b + k + 1)
                link(nc.vector.tensor_scalar(junk[:], small[:, CNT_COL:CNT_COL + DIGITS], float(CHOSEN), None,
                                             ALU.is_ge, ALU.add, accum_out=passed[:]), *first)
                link(nc.vector.scalar_tensor_tensor(base[(k + 1) % 2][:], passed[:], 16.0 ** (3 - k % 4),
                                                    base[k % 2][:], ALU.mult, ALU.add), *second)

            def round_keys(b, q):
                lg = logit[q]
                dve.wait_ge(s_logit, CHUNKS * (b + 1))
                nc.vector.tensor_tensor(tmp[0][:], rstd[1][:], small[:, LOGIT_COL:LOGIT_COL + BLOCKS], ALU.mult)
                link(nc.vector.tensor_tensor(tmp[1][:], rstd[1][:], mean[1][:], ALU.mult))
                link(nc.vector.scalar_tensor_tensor(tmp[2][:], tmp[1][:], rw_sum[:, 0:1], tmp[0][:],
                                                    ALU.mult, ALU.add))
                link(nc.vector.tensor_scalar(lg[:], tmp[2][:], rb[:, 0:1], None, ALU.add))
                bits = lg[:].bitcast(I32)
                link(nc.vector.tensor_scalar(flip[:].bitcast(I32), bits, 31, -2 ** 31,
                                             ALU.arith_shift_right, ALU.bitwise_or))
                link(nc.vector.tensor_tensor(key[:].bitcast(I32), bits, flip[:].bitcast(I32), ALU.bitwise_xor))
                nc.vector.tensor_scalar(key_hi[:], key[:], 16, None, ALU.logical_shift_right)
                link(nc.vector.tensor_scalar(key_lo[:], key[:], 0xFFFF, None, ALU.bitwise_and))
                nc.vector.memset(base[0][:], 0.0)
                link(nc.vector.tensor_copy(digit_key[:], key_hi[:]))

            def stage(p, job):
                kind, off, k = job
                b, q = p.image(off)
                if kind == "N1":
                    block_stats(0, b, q, k)
                elif kind == "N2":
                    for i in range(2):
                        block_stats(1, b, q, 2 * k + i)
                elif kind == "N1M":
                    moments(0, EPS_C)
                    nc.vector.scalar_tensor_tensor(offset1[:], mean[0][:], -1.0, rstd[0][:],
                                                   ALU.mult, ALU.mult).then_inc(s_mom, 1)
                elif kind == "SE1":
                    dve.wait_ge(s_pool, b + 1)
                    nc.vector.tensor_reduce(
                        pooled[:], small[:, POOL_COL:POOL_COL + 2 * BLOCKS].rearrange("p (h j) -> p h j", h=HALVES),
                        AX_X, ALU.add).then_inc(s_pooled, 1)
                elif kind == "SE2":
                    dve.wait_ge(s_hidr, b + 1)
                    nc.vector.tensor_scalar(hid4[:], group_mask[:], hid[:, 0:1], None, ALU.mult).then_inc(s_hid4, 1)
                elif kind == "SE3":
                    dve.wait_ge(s_se, b + 1)
                    nc.vector.tensor_tensor(
                        pre[:], small[:, SE_COL + 1:SE_COL + 1 + 2 * KGROUPS].rearrange("p (h k) -> p h k", h=HALVES),
                        cb2[:], ALU.add).then_inc(s_pre, 1)
                elif kind == "SE4":
                    dve.wait_ge(s_delta, b + 1)
                    nc.vector.tensor_scalar(coef[:, :, 0], delta[:, :, 0], 1.0, None, ALU.add)
                    nc.vector.tensor_copy(coef[:, :, 2], delta[:, :, 2])
                    link(nc.vector.tensor_scalar(coef[:, :, 1], delta[:, :, 1], 0.5, 1.0, ALU.mult, ALU.add))
                    nc.vector.scalar_tensor_tensor(coef[:, :, 3], delta[:, :, 3], 0.5, coef[:, :, 1],
                                                   ALU.mult, ALU.subtract).then_inc(s_coef, 1)
                elif kind == "CV":
                    larger = []
                    for h in range(HALVES):
                        dve.wait_ge(s_branch, 2 * CHUNKS * b + 2 * k + h + 1)
                        at = p.bank(job, h)[:]
                        larger.append(mark(nc.vector.scalar_tensor_tensor(
                            at, at, coef[:, h, 0:1], branch[h][:], ALU.mult, ALU.max)))
                    for h in range(HALVES):
                        at = X[:, h, tokens(k)]
                        dve.wait_ge(s_chain, larger[h])
                        nc.vector.scalar_tensor_tensor(at, p.bank(job, h)[:], coef[:, h, 1:2], at,
                                                       ALU.add, ALU.add).then_inc(s_x2, 1)
                elif kind == "N2M":
                    moments(1, EPS_T)
                    m, r, inv = mean[1][:], rstd[1][:], tmp[0][:]
                    nc.vector.scalar_tensor_tensor(z_offset[:], m, -1.0, r, ALU.mult, ALU.mult)
                    link(nc.vector.tensor_scalar(z_scale[:], r, 1.0, None, ALU.add))
                    link(nc.vector.reciprocal(inv, z_scale[:]))
                    link(nc.vector.tensor_tensor(T[q][:, :, C + 1], r, inv, ALU.mult))
                    nc.vector.scalar_tensor_tensor(T[q][:, :, C], m, -1.0, T[q][:, :, C + 1], ALU.mult, ALU.mult)
                    round_keys(b, q)
                elif kind == "TK":
                    z = [z_row(q, 4 * k + i) for i in range(4)]
                    if k:
                        digit_found(b, k - 1, z[0:1], z[1:2] if k != ROUNDS // 2 else ())
                    else:
                        z[0](), z[1]()
                    if k == ROUNDS // 2:
                        nc.vector.tensor_scalar(tmp[1][:], digit_key[:], base[0][:, 0:1], 70000.0,
                                                ALU.is_gt, ALU.mult)
                        link(nc.vector.tensor_scalar(tmp[0][:], digit_key[:], base[0][:, 0:1], None, ALU.is_equal),
                             z[1])
                        link(nc.vector.scalar_tensor_tensor(tmp[2][:], key_lo[:], 1.0, tmp[0][:],
                                                            ALU.add, ALU.mult))
                        nc.vector.tensor_tensor(low_key[:], tmp[2][:], tmp[1][:], ALU.add)
                        link(nc.vector.memset(base[0][:], 1.0))
                    src = digit_key if k < ROUNDS // 2 else low_key
                    link(nc.vector.tensor_scalar(tried[:], digits[:], 16.0 ** (3 - k % 4), base[k % 2][:, 0:1],
                                                 ALU.mult, ALU.add), z[2])
                    link(nc.vector.tensor_tensor(
                        above[:], src[:].unsqueeze(1).to_broadcast([P, DIGITS, BLOCKS]),
                        tried[:].unsqueeze(2).to_broadcast([P, DIGITS, BLOCKS]), ALU.is_ge), z[3])
                    with nc.allow_low_precision("counts up to 32 are exact in bfloat16"):
                        nc.vector.tensor_reduce(count[:], above[:], AX_X, ALU.add).then_inc(s_cnt, 1)
                elif kind == "RANK1":
                    digit_found(b, ROUNDS - 1, (), ())
                    nc.vector.tensor_scalar(gt_eq[:, 0, :], low_key[:], base[0][:, 0:1], None, ALU.is_gt)
                    nc.vector.tensor_scalar(gt_eq[:, 1, :], low_key[:], base[0][:, 0:1], None,
                                            ALU.is_equal).then_inc(s_cnt, 1)
                elif kind == "RANK2":
                    dve.wait_ge(s_tot, (ROUNDS + 1) * (b + 1))
                    for i in range(2):
                        n = RANK_COL + (2 + i) * BLOCKS
                        ins = nc.vector.tensor_tensor_scan(incl[i][:], ones_row[:], small[:, n:n + BLOCKS], 0.0,
                                                           ALU.mult, ALU.add)
                    link(ins)
                    nc.vector.tensor_scalar(need[:], incl[0][:, BLOCKS - 1:BLOCKS], -1.0, float(CHOSEN),
                                            ALU.mult, ALU.add)
                    for i in range(2):
                        n = RANK_COL + (2 + i) * BLOCKS
                        ins = nc.vector.tensor_tensor(tmp[i][:], incl[i][:], small[:, n:n + BLOCKS], ALU.subtract)
                    link(ins)
                    for i in range(2):
                        n = RANK_COL + i * BLOCKS
                        ins = nc.vector.tensor_tensor(before[i][:], tmp[i][:], small[:, n:n + BLOCKS], ALU.add)
                    link(ins)
                    nc.vector.scalar_tensor_tensor(tmp[0][:], before[1][:], need[:, 0:1], gt_eq[:, 1, :],
                                                   ALU.is_lt, ALU.mult)
                    link(nc.vector.scalar_tensor_tensor(tmp[1][:], before[1][:], need[:, 0:1], before[0][:],
                                                        ALU.min, ALU.add))
                    link(nc.vector.tensor_tensor(chosen[:], tmp[0][:], gt_eq[:, 0, :], ALU.add))
                    nc.vector.tensor_tensor(logit[q][:], logit[q][:], chosen[:], ALU.mult)
                    link(nc.vector.tensor_scalar(tmp[2][:], chosen[:], -float(TOKENS), float(TOKENS),
                                                 ALU.mult, ALU.add))
                    nc.vector.tensor_tensor(index[q][:], tmp[2][:], tmp[1][:], ALU.add).then_inc(s_index, 1)
                elif kind == "FN":
                    dve.wait_ge(s_back[k % 2], DMA * 4 * (CHUNKS // 2 * b + k // 2 + 1))
                    for j in range(4 * k, 4 * k + 4):
                        row = T[q][:, j, 0:C]
                        ins = nc.vector.scalar_tensor_tensor(row, y_back[:, 4 * (k % 2) + j % 4, :],
                                                             logit[q][:, j:j + 1], row, ALU.mult, ALU.add)
                    ins.then_inc(s_added, 1)

            def copy_y(b, q, f):
                dve.wait_ge(s_mm2, FCHUNKS * b + f + 1)
                if type(b) is not int or FCHUNKS * b + f > 0:
                    dve.wait_ge(s_ytab[(f - 1) % FCHUNKS], DMA * (b + (1 if f else 0)))
                for i in range(2):
                    ins = nc.vector.tensor_tensor(
                        y_rows[:, 2 * i:2 * i + 2, :], y_ps[i][:].rearrange("p (j c) -> p j c", j=2),
                        fb2[:].unsqueeze(1).to_broadcast([P, 2, C]), ALU.add)
                ins.then_inc(s_y, 1)

            def period(p):
                ffn = 0 in p.offsets
                if p.full:
                    chain.setdefault("first", chain["before"] + chain["here"])
                    chain["before"] = chain["first"] + chain.get("each", 0) * (p.b - FIRST_FULL)
                    chain["here"] = 0
                elif p.b == IMAGES - 2:
                    chain["before"], chain["here"] = chain["first"] + chain["each"] * N_FULL, 0
                for s in range(STEPS):
                    if ffn and s % HB == 0:
                        for h in range(HALVES):
                            dve.wait_ge(s_xshi, 2 * FCHUNKS * p.b + 2 * (s // HB) + h + 1)
                            nc.vector.tensor_tensor(xs_lo[:, h, :], p.bank(("XS", 0, s // HB), h)[:],
                                                    xs_hi[:, h, :].bitcast(F32), ALU.subtract).then_inc(s_xslo, 1)
                    for job in p.jobs("DVE", 2 * s):
                        stage(p, job)
                    if ffn:
                        dve.wait_ge(s_g, STEPS * p.b + s + 1)
                        r = g_place(p.q, s)
                        nc.vector.tensor_tensor(g_lo[r][:], h_ps[s % 2][:], g_hi[r][:].bitcast(F32),
                                                ALU.subtract).then_inc(s_glo, 1)
                    for job in p.jobs("DVE", 2 * s + 1):
                        stage(p, job)
                    if s % HB == 1 and (0 if s > HB else -1) in p.offsets:
                        copy_y(*p.image(0 if s > HB else -1), (s // HB - 1) % FCHUNKS)
                if p.full:
                    chain["each"] = chain["here"]

            run(dve, period)


def kernel(x, L0_conv_w1, L0_conv_b1, L0_conv_w2, L0_conv_b2, L0_ffn_attention_mask, L0_ffn_wr, L0_ffn_br,
           L0_ffn_w1, L0_ffn_b1, L0_ffn_w2, L0_ffn_b2):
    import concourse.bacc as bacc
    import numpy as np
    from concourse.bass_utils import run_bass_kernel_spmd

    images, channels, height, width = x.shape
    relu_h = L0_conv_w1.shape[0]
    groups = P // relu_h
    a = {k: np.asarray(v) for k, v in (
        ("w1", L0_conv_w1), ("b1", L0_conv_b1), ("w2", L0_conv_w2), ("b2", L0_conv_b2), ("wr", L0_ffn_wr),
        ("br", L0_ffn_br), ("f1", L0_ffn_w1), ("fb1", L0_ffn_b1), ("f2", L0_ffn_w2), ("fb2", L0_ffn_b2))}
    digits = 15
    consts = np.zeros((P, 2 * P + digits + groups), np.float32)
    consts[:, 0:P] = np.eye(P)
    consts[:, P:2 * P] = np.triu(np.ones((P, P)), 1)
    consts[:, 2 * P:2 * P + digits] = np.arange(1, digits + 1)
    consts[:, 2 * P + digits:] = np.kron(np.eye(groups), np.ones((relu_h, 1)))
    arrays = {
        "x": np.asarray(x).reshape(images, channels, height * width),
        "conv_w1": np.tile(a["w1"].T, (1, groups)),
        "conv_b1": np.tile(a["b1"], groups)[:, None],
        "conv_w2": a["w2"].reshape(2, channels, 2, relu_h).transpose(0, 2, 3, 1).reshape(P, channels),
        "conv_b2": a["b2"].reshape(2, channels // P, P, 2).transpose(2, 1, 0, 3).reshape(P, -1, groups),
        "router_w": a["wr"].reshape(-1, P).T,
        "router_b": np.tile(a["br"], P)[:, None],
        "ffn_w1": a["f1"],
        "ffn_b1": a["fb1"].reshape(-1, P).T,
        "ffn_w2": a["f2"],
        "ffn_b2": np.tile(a["fb2"], (P, 1)),
        "consts": consts,
    }
    arrays = {k: np.ascontiguousarray(v) for k, v in arrays.items()}
    from concourse import mybir as _mybir

    nc = bacc.Bacc("TRN2", target_bir_lowering=False, num_devices=1, dynamic_dma_scratch_size=4096)
    args = {k: nc.dram_tensor(k, v.shape, _mybir.dt.from_np(v.dtype), kind="ExternalInput").ap()
            for k, v in arrays.items()}
    out = nc.dram_tensor("out", arrays["x"].shape, F32, kind="ExternalOutput").ap()
    metaformer_kernel(nc, out=out, **args)
    r = run_bass_kernel_spmd(nc, [arrays], core_ids=[0])
    return r.results[0]["out"].reshape(images, channels, height, width)
```

```python
from contextlib import ExitStack

from concourse import mybir
from concourse.bass import IndirectOffsetOnAxis

ALU = mybir.AluOpType
ACT = mybir.ActivationFunctionType
F32 = mybir.dt.float32
F32R = mybir.dt.float32r
BF16 = mybir.dt.bfloat16
I32 = mybir.dt.int32
U32 = mybir.dt.uint32
AX_X = mybir.AxisListType.X

P = 128
DMA = 16
LAG = 2
G_RING = 3
AUX = 3
TURN = 3
OUT_RING = 2
EPS_C = 1e-6
EPS_T = 1e-5


AT = dict(CV=-6, CVd=2, N2=-4.5, N2d=2, N2M=10, TK=12, TKd=1, RANK=20, SC=21.5, SCd=0.8, FN=0.5, FNd=2.1,
          N1=1.5, N1d=2, N1M=16, NORM=16.5, NORMd=0.5, SE=23.5, N1s=0, FNl=1.5, TKl=0.5)


def plan(chunks, steps):
    slots = {e: [[] for _ in range(2 * steps)] for e in ("SP", "POOL", "PE", "ACT", "DVE")}

    def put(stage, off, k, **at):
        for engine, step in at.items():
            periods, slot = divmod(int(round(2 * step)), 2 * steps)
            slots[engine][slot].append((stage, off - periods, k))

    for k in range(chunks):
        t = AT["CV"] + AT["CVd"] * k
        put("CV", 1, k, PE=t, ACT=t, DVE=t + 0.5)
    for k in range(chunks):
        t = AT["N2"] + AT["N2d"] * k
        put("N2", 1, k, PE=t, ACT=t, DVE=t + 0.5)
        put("LOAD", 2, k, SP=max(t, 0))
    for i in range(4):
        put("N2M", 1, i, DVE=AT["N2M"] + 0.5 * i)
    for r in range(8):
        t = AT["TK"] + AT["TKd"] * r
        put("TK", 1, r, DVE=t)
    put("RANK1", 1, 0, DVE=AT["RANK"], PE=AT["RANK"] + 0.5)
    for i in range(2):
        put("RANK2", 1, i, DVE=AT["RANK"] + 1 + 0.5 * i)
    for c in range(chunks):
        t = AT["FN"] + AT["FNd"] * c
        put("FN", -1, c, POOL=t - 2, DVE=t - AT["FNl"], PE=t, ACT=t, SP=t)
    for g in range(2 * chunks):
        t = AT["N1"] + AT["N1d"] * (g // 2) + AT["N1s"] * (g % 2)
        put("N1", 2, g, PE=t, ACT=t, DVE=t + 0.5)
    for i in range(2):
        put("N1M", 2, i, DVE=AT["N1M"] + 0.5 * i)
    for k in range(chunks):
        t = AT["NORM"] + AT["NORMd"] * k
        put("NORM", 2, k, ACT=t, DVE=t, POOL=t + 0.5)
    for c in range(chunks):
        put("SC", 1, c, POOL=AT["SC"] + AT["SCd"] * c)
    for r in range(8):
        put("TK", 1, r, PE=AT["TK"] + AT["TKd"] * r + AT["TKl"])
    t = AT["SE"]
    put("SUM", 2, 0, PE=t - 0.5)
    put("SE1", 2, 0, DVE=t, PE=t + 0.5, ACT=t + 0.5)
    put("SE2", 2, 0, DVE=t + 1, PE=t + 1.5)
    put("SE3", 2, 0, DVE=t + 2, ACT=t + 2)
    put("SE4", 2, 0, DVE=t + 2.5)
    return slots


def bank_uses(plan_, steps, steps_of_chunk, offsets):
    uses = []
    for s in range(steps):
        if 0 in offsets and s % steps_of_chunk == 0:
            uses += [("XS", 0, s // steps_of_chunk, h) for h in range(2)]
        for job in plan_["PE"][2 * s] + plan_["PE"][2 * s + 1]:
            if job[1] in offsets:
                uses += [job + (h,) for h in range({"N1": 1, "N2": 2, "CV": 2, "FN": 2}.get(job[0], 0))]
    return uses


def metaformer_kernel(nc, x, conv_w1, conv_b1, conv_w2, conv_b2, router_w, router_b, ffn_w1, ffn_b1,
                      ffn_w2, ffn_b2, consts, out):
    IMAGES, C, TOKENS = x.shape
    H = ffn_w1.shape[1]
    HALVES = C // P
    BLOCKS = TOKENS // P
    CHUNK = 512
    CHUNKS = TOKENS // CHUNK
    SLOTS = TOKENS // 2
    CHOSEN = SLOTS - 1
    FCHUNKS = SLOTS // CHUNK
    HB = H // P
    STEPS = FCHUNKS * HB
    KGROUPS = 4
    RELU_H = P // KGROUPS
    DIGITS = 15
    ROUNDS = 8
    assert IMAGES > 2 * TURN
    ROW = C + 2
    PLAN = plan(CHUNKS, STEPS)

    xT = x.rearrange("b (h p) t -> b p h t", p=P)
    oT = out.rearrange("b (h p) t -> b p h t", p=P)

    ctx = ExitStack()
    with ctx:
        def sb(name, shape, dt):
            return ctx.enter_context(nc.sbuf_tensor(name, shape, dt))

        def sem(name):
            return ctx.enter_context(nc.semaphore(name))

        X = sb("X", [P, HALVES, TOKENS], F32)
        T = [sb(f"T{q}", [P, BLOCKS, ROW], F32) for q in range(TURN)]
        out_sb = [sb(f"out_sb{r}", [P, CHUNK], F32) for r in range(OUT_RING)]
        w1_hi = sb("w1_hi", [P, HALVES, H], F32R)
        w1_lo = sb("w1_lo", [P, HALVES, H], F32R)
        w2_hi = sb("w2_hi", [P, HB, C], F32R)
        w2_lo = sb("w2_lo", [P, HB, C], F32R)
        g_hi = [sb(f"g_hi{r}", [P, CHUNK], F32R) for r in range(G_RING)]
        g_lo = [sb(f"g_lo{r}", [P, CHUNK], F32R) for r in range(G_RING)]
        rows = sb("rows", [P, 4, ROW], F32)
        xs_hi = sb("xs_hi", [P, HALVES, CHUNK], F32R)
        xs_lo = sb("xs_lo", [P, HALVES, CHUNK], F32R)
        y_rows = sb("y_rows", [P, 4, C], F32)
        y_back = sb("y_back", [P, 8, C], F32)
        branch = [sb(f"branch{r}", [P, CHUNK], F32) for r in range(2)]
        ident = sb("ident", [P, P], F32)
        tri = sb("tri", [P, P], BF16)
        digits = sb("digits", [P, 4, DIGITS], F32)
        ones_f = sb("ones_f", [P, 1], F32)
        ones_b = sb("ones_b", [P, P], BF16)
        cw1 = sb("cw1", [P, HALVES, P], F32)
        cb1 = sb("cb1", [P, 1], F32)
        cw2 = sb("cw2", [P, C], F32)
        cb2 = sb("cb2", [P, HALVES, KGROUPS], F32)
        rw = sb("rw", [P, HALVES], F32)
        rb = sb("rb", [P, 1], F32)
        rw_sum = sb("rw_sum", [P, 1], F32)
        fb1 = sb("fb1", [P, HB], F32)
        fb2 = sb("fb2", [P, C], F32)
        stats = [sb(f"stats{n}", [P, BLOCKS, 6], F32) for n in range(2)]
        norm_tmp = [sb(f"norm_tmp{i}", [P, BLOCKS], F32) for i in range(4)]
        tmp = [sb(f"tmp{i}", [P, BLOCKS], F32) for i in range(3)]
        offset1 = sb("offset1", [P, BLOCKS], F32)
        mean = [sb(f"mean{n}", [P, BLOCKS], F32) for n in range(2)]
        rstd = [sb(f"rstd{n}", [P, BLOCKS], F32) for n in range(2)]
        z_scale = sb("z_scale", [P, BLOCKS], F32)
        z_offset = sb("z_offset", [P, BLOCKS], F32)
        acc = sb("acc", [P, 4, C], F32)
        pooled = sb("pooled", [P, HALVES], F32)
        hid = sb("hid", [P, 1], F32)
        group_mask = sb("group_mask", [P, KGROUPS], F32)
        hid4 = sb("hid4", [P, KGROUPS], F32)
        pre = sb("pre", [P, HALVES, KGROUPS], F32)
        delta = sb("delta", [P, HALVES, KGROUPS], F32)
        coef = sb("coef", [P, HALVES, KGROUPS], F32)
        logit = [sb(f"logit{q}", [P, BLOCKS], F32) for q in range(TURN)]
        index = [sb(f"index{q}", [P, BLOCKS], U32) for q in range(TURN)]
        key_lo = sb("key_lo", [P, BLOCKS], U32)
        digit_key = sb("digit_key", [P, BLOCKS], F32)
        low_key = sb("low_key", [P, BLOCKS], F32)
        base = [sb(f"base{i}", [P, 1], F32) for i in range(2)]
        above = sb("above", [P, DIGITS, BLOCKS], BF16)
        count = sb("count", [P, DIGITS], BF16)
        junk = sb("junk", [P, DIGITS], F32)
        passed = sb("passed", [P, 1], F32)
        gt_eq = sb("gt_eq", [P, 2, BLOCKS], BF16)
        incl = [sb(f"incl{i}", [P, BLOCKS], F32) for i in range(2)]
        before = [sb(f"before{i}", [P, BLOCKS], F32) for i in range(2)]
        need = sb("need", [P, 1], F32)
        chosen = incl[0]
        ones_row = sb("ones_row", [P, BLOCKS], F32)

        psum = [ctx.enter_context(nc.psum_tensor(f"psum{i}", [P, 512], F32)) for i in range(8)]
        y_ps, h_ps, aux_ps, small = psum[0:2], psum[2:4], psum[4:4 + AUX], psum[7]
        POOL_COL, LOGIT_COL, SE_COL, CNT_COL, RANK_COL = 0, 64, 96, 112, 128
        RWS_COL = 300
        x_table = [nc.dram_tensor(f"x_table{q}", (SLOTS, ROW), F32).ap() for q in range(TURN)]
        y_table = [nc.dram_tensor(f"y_table{q}", (SLOTS, C), F32).ap() for q in range(TURN)]

        s_const = sem("s_const")
        s_met = sem("s_met")
        s_wload = sem("s_wload")
        s_zero = sem("s_zero")
        s_zrow = sem("s_zrow")
        s_wsplit = sem("s_wsplit")
        s_rws = sem("s_rws")
        s_xin = [sem(f"s_xin{k}") for k in range(CHUNKS)]
        s_out = [sem(f"s_out{r}") for r in range(OUT_RING)]
        s_tok = [sem(f"s_tok{n}") for n in range(2)]
        s_copied = [sem(f"s_copied{n}") for n in range(2)]
        s_mom = sem("s_mom")
        s_norm = [sem(f"s_norm{i}") for i in range(2)]
        s_acc = sem("s_acc")
        s_pool = sem("s_pool")
        s_pooled = sem("s_pooled")
        s_hid = sem("s_hid")
        s_hidr = sem("s_hidr")
        s_se = sem("s_se")
        s_pre = sem("s_pre")
        s_delta = sem("s_delta")
        s_coef = sem("s_coef")
        s_cv = sem("s_cv")
        s_branch = sem("s_branch")
        s_logit = sem("s_logit")
        s_cnt = sem("s_cnt")
        s_tot = sem("s_tot")
        s_before = sem("s_before")
        s_index = sem("s_index")
        s_scat = sem("s_scat")
        s_rows = sem("s_rows")
        s_cn = sem("s_cn")
        s_xs = sem("s_xs")
        s_xshi = sem("s_xshi")
        s_h = sem("s_h")
        s_g = sem("s_g")
        s_glo = sem("s_glo")
        s_mm2 = sem("s_mm2")
        s_y = sem("s_y")
        s_ytab = [sem(f"s_ytab{f}") for f in range(FCHUNKS)]
        s_back = [sem(f"s_back{i}") for i in range(2)]
        s_added = sem("s_added")
        s_fn = sem("s_fn")
        s_hid4 = sem("s_hid4")
        s_max = sem("s_max")
        s_x2 = sem("s_x2")
        s_outc = sem("s_outc")
        s_xslo = sem("s_xslo")
        s_chain = sem("s_chain")


        block = ctx.enter_context(nc.Block())
        FULL = (-1, 0, 1, 2)
        TAIL = 8
        FIRST_FULL, N_FULL = 1, IMAGES - TURN

        class Period:

            def __init__(self, b, q, offsets, before, used):
                self.b, self.q, self.offsets = b, q, offsets
                self.full = offsets == FULL
                self.uses = bank_uses(PLAN, STEPS, HB, offsets)
                self.before = before
                self.used = used

            def image(self, off):
                return self.b + off, (self.q + off) % TURN

            def jobs(self, engine, slot):
                return [job for job in PLAN[engine][slot] if job[1] in self.offsets]

            def tail(self):
                return [(kind, off - 1, k, h) for kind, off, k, h in (self.before + self.uses)[-TAIL:]]

            def index(self, use):
                if use in self.uses:
                    return self.uses.index(use)
                return self.before.index(use) - len(self.before)

            def bank(self, job, h=0):
                return aux_ps[(self.used + self.index(job + (h,))) % AUX]

            def bank_before(self, use):
                n = len(self.before) + self.uses.index(use) - AUX
                return (self.before + self.uses)[n] if n >= 0 else None

        def run(eng, period):
            used, tail = 0, []
            for b, offsets in ((-2, (2,)), (-1, (1, 2)), (0, (0, 1, 2))):
                p = Period(b, b % TURN, offsets, tail, used)
                period(p)
                used, tail = used + len(p.uses), p.tail()
            full = Period(None, 0, FULL, tail, used)
            assert full.tail() == tail and len(full.uses) % AUX == 0
            peeled = (N_FULL - 1) % TURN + 1
            for b in range(FIRST_FULL, FIRST_FULL + peeled):
                period(Period(b, b % TURN, FULL, tail, used))
            b0 = FIRST_FULL + peeled
            with eng.Fori(0, (N_FULL - peeled) // TURN) as i:
                for k in range(TURN):
                    b = nc.snap(i * TURN + (b0 + k), engines=[eng.engine], min_val=b0 + k, max_val=IMAGES - TURN)
                    period(Period(b, (b0 + k) % TURN, FULL, tail, used))
            for b, offsets in ((IMAGES - 2, (-1, 0, 1)), (IMAGES - 1, (-1, 0)), (IMAGES, (-1,))):
                p = Period(b, b % TURN, offsets, tail, used)
                period(p)
                used, tail = used + len(p.uses), p.tail()

        def settled(eng):
            eng.sem_inc(s_met, 1)

        def tokens(k, n=CHUNK):
            return slice(k * n, (k + 1) * n)

        def g_place(q, s):
            return (q * STEPS + s) % G_RING

        stage_area = T[1][:].rearrange("p j c -> p (j c)")
        w1_raw = stage_area[:, 0:HALVES * H].rearrange("p (h m) -> p h m", h=HALVES)
        w2_raw = stage_area[:, HALVES * H:HALVES * H + HB * C].rearrange("p (h c) -> p h c", h=HB)
        ones_sq = stage_area[:, 6 * H:6 * H + P]
        tri_f = stage_area[:, 6 * H + P:6 * H + 2 * P]

        @block.sync
        def _(sp):
            for dst, src in ((ident[:], consts[:, 0:P]), (tri_f, consts[:, P:2 * P]),
                             (digits[:].rearrange("p k d -> p (k d)"), consts[:, 2 * P:2 * P + 4 * DIGITS]),
                             (group_mask[:], consts[:, 2 * P + 4 * DIGITS:2 * P + 4 * DIGITS + KGROUPS]),
                             (cw1[:], conv_w1.rearrange("(h p) m -> p h m", p=P)), (cb1[:], conv_b1),
                             (cw2[:], conv_w2), (cb2[:], conv_b2), (rw[:], router_w), (rb[:], router_b),
                             (fb1[:], ffn_b1), (fb2[:], ffn_b2)):
                sp.dma_start(dst, src).then_inc(s_const, DMA)
            sp.dma_start(w1_raw, ffn_w1.rearrange("(h p) m -> p h m", p=P)).then_inc(s_wload, DMA)
            sp.dma_start(w2_raw, ffn_w2.rearrange("(h p) m -> p h m", p=P)).then_inc(s_wload, DMA)
            sp.wait_ge(s_zero, 2)
            for q in range(TURN):
                sp.dma_start(x_table[q][SLOTS - 1:SLOTS, 0:C], y_back[0:1, 0, :]).then_inc(s_zrow, DMA)
                sp.dma_start(x_table[q][SLOTS - 1:SLOTS, C:ROW], y_back[0:1, 1, 0:2]).then_inc(s_zrow, DMA)
            sp.wait_ge(s_zrow, 2 * TURN * DMA)

            def period(p):
                for s in range(STEPS):
                    if s % HB == 1 and (0 if s > HB else -1) in p.offsets:
                        b, q = p.image(0 if s > HB else -1)
                        f = (s // HB - 1) % FCHUNKS
                        sp.wait_ge(s_y, FCHUNKS * b + f + 1)
                        settled(sp)
                        sp.dma_start(y_table[q][f * CHUNK:(f + 1) * CHUNK, :].rearrange("(p i) c -> p i c", i=4),
                                     y_rows[:]).then_inc(s_ytab[f], DMA)
                    for kind, off, k in p.jobs("SP", 2 * s) + p.jobs("SP", 2 * s + 1):
                        b, q = p.image(off)
                        if kind == "LOAD":
                            if type(b) is not int or b > 0:
                                sp.wait_ge(s_logit, CHUNKS * (b - 1) + k + 1)
                                settled(sp)
                            sp.dma_start(X[:, :, tokens(k)], xT[b, :, :, tokens(k)]).then_inc(s_xin[k], DMA)
                        elif kind == "FN":
                            for h in range(HALVES):
                                r = (HALVES * k + h) % OUT_RING
                                sp.wait_ge(s_outc, HALVES * CHUNKS * b + HALVES * k + h + 1)
                                settled(sp)
                                sp.dma_start(oT[b, :, h, tokens(k)], out_sb[r][:]).then_inc(s_out[r], DMA)
                if 1 in p.offsets:
                    b, q = p.image(1)
                    if 0 in p.offsets:
                        sp.wait_ge(s_xs, 2 * FCHUNKS * b)
                        settled(sp)
                    sp.wait_ge(s_scat, DMA * BLOCKS * (b + 1))
                    settled(sp)
                    sp.dma_start(rows[:], x_table[q][0:CHUNK, :].rearrange("(p i) c -> p i c", i=4)
                                 ).then_inc(s_rows, DMA)

            run(sp, period)
            for r in range(OUT_RING):
                sp.wait_ge(s_out[r], DMA * HALVES * CHUNKS // OUT_RING * IMAGES)

        @block.gpsimd
        def _(pool):
            nc.gpsimd.memset(y_back[:], 0.0).then_inc(s_zero, 1)

            def period(p):
                for slot in range(2 * STEPS):
                    for kind, off, k in p.jobs("POOL", slot):
                        b, q = p.image(off)
                        if kind == "FN":
                            known = min(CHUNK * (k + 1), SLOTS)
                            pool.wait_ge(s_ytab[min(k, FCHUNKS - 1)], DMA * (b + 1))
                            settled(pool)
                            if type(b) is not int or CHUNKS * b + k - 1 > 0:
                                pool.wait_ge(s_added, CHUNKS * b + k - 1)
                                settled(pool)
                            for i in range(4):
                                j = 4 * k + i
                                pool.indirect_dma_start(
                                    y_back[:, 4 * (k % 2) + i, :], None, y_table[q][0:known, :],
                                    IndirectOffsetOnAxis(ap=index[q][:, j:j + 1], axis=0),
                                    bounds_check=min(known, CHOSEN) - 1, oob_is_err=False).then_inc(s_back[k % 2], DMA)
                        elif kind == "SC":
                            if k == 0:
                                pool.wait_ge(s_index, b + 1)
                                settled(pool)
                            for j in range(4 * k, 4 * k + 4):
                                pool.indirect_dma_start(
                                    x_table[q], IndirectOffsetOnAxis(ap=index[q][:, j:j + 1], axis=0),
                                    T[q][:, j, :], None,
                                    bounds_check=CHOSEN - 1, oob_is_err=False).then_inc(s_scat, DMA)
                        elif kind == "NORM" and k > 0:
                            for half in range(2):
                                pool.wait_ge(s_norm[half], CHUNKS * b + k + 1)
                                settled(pool)
                            if k > 1:
                                pool.wait_ge(s_acc, (CHUNKS - 1) * b + k - 1)
                                settled(pool)
                            elif type(b) is not int or b > 0:
                                pool.wait_ge(s_pool, b)
                                settled(pool)
                            first = acc[:] if k > 1 else T[q][:, 0:4, 0:C]
                            nc.gpsimd.tensor_tensor(acc[:], first, T[q][:, 4 * k:4 * k + 4, 0:C],
                                                    ALU.add).then_inc(s_acc, 1)

            run(pool, period)

        @block.tensor
        def _(pe):
            pe.wait_ge(s_const, DMA * 12)
            pe.wait_ge(s_wsplit, 1)
            for h in range(HALVES):
                rws = nc.tensor.matmul(small[:, RWS_COL:RWS_COL + 1], ones_sq, rw[:, h:h + 1],
                                       start=(h == 0), stop=(h == HALVES - 1))
            rws.then_inc(s_rws, 1)

            def flip_block(out, src, **flags):
                return nc.tensor.matmul(out, src, ident[:], is_transpose=True, skip_group_check=True, **flags)

            def bank_of(p, job, h=0):
                last = p.bank_before(job + (h,))
                if last is not None:
                    kind, off, k, i = last
                    b = p.b + off
                    if kind in ("N1", "N2"):
                        n = 2 * CHUNKS * b + (k if kind == "N1" else 2 * k + i) + 1
                        pe.wait_ge(s_copied[0 if kind == "N1" else 1], n)
                    elif kind == "CV":
                        pe.wait_ge(s_max, 2 * CHUNKS * b + 2 * k + i + 1)
                    elif kind == "FN":
                        pe.wait_ge(s_outc, 2 * CHUNKS * b + 2 * k + i + 1)
                    else:
                        pe.wait_ge(s_xslo, 2 * FCHUNKS * b + 2 * k + i + 1)
                return p.bank(job, h)

            def to_tokens(p, job, h, done, pair):
                bank = bank_of(p, job, h)
                for i in range(2):
                    for half in range(HALVES):
                        t = flip_block(bank[:, i * C + half * P:i * C + (half + 1) * P],
                                       X[:, half, tokens(2 * pair + i, P)], start=(i + half == 0), stop=True)
                t.then_inc(done, 1)

            def to_channels(p, job, h, done):
                b, q = p.image(job[1])
                bank = bank_of(p, job, h)
                for i in range(4):
                    t = flip_block(bank[:, tokens(i, P)], T[q][:, 4 * job[2] + i, h * P:(h + 1) * P],
                                   start=(i == 0), stop=True)
                t.then_inc(done, 1)

            def stage(p, job):
                kind, off, k = job
                b, q = p.image(off)
                if kind == "N1":
                    if k % 2 == 0:
                        pe.wait_ge(s_xin[k // 2], DMA * (b + 1))
                    to_tokens(p, job, 0, s_tok[0], k)
                elif kind == "SUM":
                    pe.wait_ge(s_acc, (CHUNKS - 1) * (b + 1))
                    if type(b) is not int or b > 0:
                        pe.wait_ge(s_before, b)
                    for h in range(HALVES):
                        for i in range(4):
                            m = nc.tensor.matmul(small[:, POOL_COL + h:POOL_COL + h + 1],
                                                 acc[:, i, h * P:(h + 1) * P], ones_f[:, 0:1],
                                                 start=(i == 0), stop=(i == 3))
                    m.then_inc(s_pool, 1)
                elif kind == "SE1":
                    pe.wait_ge(s_pooled, b + 1)
                    for h in range(HALVES):
                        m = nc.tensor.matmul(small[:, SE_COL:SE_COL + 1], cw1[:, h, :], pooled[:, h:h + 1],
                                             start=(h == 0), stop=(h == HALVES - 1))
                    m.then_inc(s_hid, 1)
                elif kind == "SE2":
                    pe.wait_ge(s_hid4, b + 1)
                    for h in range(HALVES):
                        col = SE_COL + 1 + KGROUPS * h
                        m = nc.tensor.matmul(small[:, col:col + KGROUPS], cw2[:, h * P:(h + 1) * P], hid4[:],
                                             start=True, stop=True)
                    m.then_inc(s_se, 1)
                elif kind == "CV":
                    for h in range(HALVES):
                        to_channels(p, job, h, s_cv)
                elif kind == "N2":
                    pe.wait_ge(s_x2, 2 * CHUNKS * b + 2 * k + 2)
                    for i in range(2):
                        to_tokens(p, job, i, s_tok[1], 2 * k + i)
                    for j in range(4 * k, 4 * k + 4):
                        for h in range(HALVES):
                            m = nc.tensor.matmul(small[:, LOGIT_COL + j:LOGIT_COL + j + 1],
                                                 X[:, h, tokens(j, P)], rw[:, h:h + 1],
                                                 start=(h == 0), stop=(h == HALVES - 1))
                    m.then_inc(s_logit, 1)
                elif kind == "TK":
                    pe.wait_ge(s_cnt, (ROUNDS + 1) * b + k + 1)
                    nc.tensor.matmul(small[:, CNT_COL:CNT_COL + DIGITS], ones_b[:], count[:],
                                     start=True, stop=True).then_inc(s_tot, 1)
                elif kind == "RANK1":
                    pe.wait_ge(s_cnt, (ROUNDS + 1) * (b + 1))
                    both = gt_eq[:].rearrange("p a j -> p (a j)")
                    nc.tensor.matmul(small[:, RANK_COL:RANK_COL + 2 * BLOCKS], tri[:], both,
                                     start=True, stop=True)
                    nc.tensor.matmul(small[:, RANK_COL + 2 * BLOCKS:RANK_COL + 4 * BLOCKS], ones_b[:], both,
                                     start=True, stop=True).then_inc(s_tot, 1)
                elif kind == "FN":
                    pe.wait_ge(s_added, CHUNKS * b + k + 1)
                    for h in range(HALVES):
                        to_channels(p, job, h, s_fn)

            def first_product(p, s):
                h, bank = s % HB, h_ps[s % 2]
                if s % HB == 0:
                    pe.wait_ge(s_xslo, 2 * FCHUNKS * p.b + 2 * (s // HB) + 2)
                if s >= 2 or -1 in p.offsets:
                    pe.wait_ge(s_glo, STEPS * p.b + s - 1)
                n = 0
                for half in range(HALVES):
                    for w, v in ((w1_hi, xs_hi), (w1_lo, xs_hi), (w1_hi, xs_lo)):
                        m = nc.tensor.matmul(bank[:], w[:, half, h * P:(h + 1) * P], v[:, half, :],
                                             start=(n == 0), stop=(n == 5))
                        n += 1
                m.then_inc(s_h, 1)

            def second_product(b, q, s):
                h, f, r = s % HB, s // HB, g_place(q, s)
                pe.wait_ge(s_glo, STEPS * b + s + 1)
                if h == 0 and (type(b) is not int or FCHUNKS * b + f > 0):
                    pe.wait_ge(s_y, FCHUNKS * b + f)
                for i in range(4):
                    for n, (g, w) in enumerate(((g_hi, w2_hi), (g_lo, w2_hi), (g_hi, w2_lo))):
                        m = nc.tensor.matmul(y_ps[i // 2][:, (i % 2) * C:(i % 2 + 1) * C],
                                             g[r][:, tokens(i, P)], w[:, h, :],
                                             start=(h == 0 and n == 0 and i % 2 == 0),
                                             stop=(h == HB - 1 and n == 2), skip_group_check=True)
                if h == HB - 1:
                    m.then_inc(s_mm2, 1)

            def period(p):
                ffn = 0 in p.offsets
                for s in range(STEPS):
                    if ffn and s % HB == 0:
                        f = s // HB
                        pe.wait_ge(s_cn, FCHUNKS * p.b + f + 1)
                        for h in range(HALVES):
                            bank = bank_of(p, ("XS", 0, f), h)
                            for i in range(4):
                                t = flip_block(bank[:, tokens(i, P)], rows[:, i, h * P:(h + 1) * P],
                                               start=(i == 0), stop=True)
                            t.then_inc(s_xs, 1)
                    if ffn and s % HB:
                        first_product(p, s)
                    for job in p.jobs("PE", 2 * s):
                        stage(p, job)
                    if s < LAG and -1 in p.offsets:
                        second_product(*p.image(-1), STEPS + s - LAG)
                    if s >= LAG and ffn:
                        second_product(*p.image(0), s - LAG)
                    if ffn and s % HB == 0:
                        first_product(p, s)
                    for job in p.jobs("PE", 2 * s + 1):
                        stage(p, job)

            run(pe, period)

        @block.scalar
        def _(act):
            def stage(p, job):
                kind, off, k = job
                b, q = p.image(off)
                if kind in ("N1", "N2"):
                    for i in range(1 if kind == "N1" else 2):
                        n = k if kind == "N1" else 2 * k + i
                        which = 0 if kind == "N1" else 1
                        act.wait_ge(s_tok[which], BLOCKS // 2 * b + n + 1)
                        nc.scalar.copy(T[q][:, 2 * n:2 * n + 2, 0:C],
                                       p.bank(job, i)[:].rearrange("p (j c) -> p j c", j=2)
                                       ).then_inc(s_copied[which], 1)
                elif kind == "NORM":
                    if k == 0:
                        act.wait_ge(s_mom, b + 1)
                    for j in range(4 * k, 4 * k + 2):
                        row = T[q][:, j, 0:C]
                        a = nc.scalar.activation(row, row, ACT.Identity, bias=offset1[:, j:j + 1],
                                                 scale=rstd[0][:, j:j + 1])
                    a.then_inc(s_norm[0], 1)
                elif kind == "SE1":
                    act.wait_ge(s_hid, b + 1)
                    nc.scalar.activation(hid[:], small[:, SE_COL:SE_COL + 1], ACT.Relu, bias=cb1[:, 0:1],
                                         scale=1.0 / TOKENS).then_inc(s_hidr, 1)
                elif kind == "SE3":
                    act.wait_ge(s_pre, b + 1)
                    nc.scalar.activation(delta[:], pre[:], ACT.Tanh, scale=0.5).then_inc(s_delta, 1)
                elif kind == "CV":
                    if k == 0:
                        act.wait_ge(s_coef, b + 1)
                    for h in range(HALVES):
                        act.wait_ge(s_cv, 2 * CHUNKS * b + 2 * k + h + 1)
                        if k:
                            act.wait_ge(s_x2, 2 * CHUNKS * b + 2 * k + h - 1)
                        nc.scalar.activation(branch[h][:], p.bank(job, h)[:], ACT.Identity,
                                             bias=coef[:, h, 3:4], scale=coef[:, h, 2:3]).then_inc(s_branch, 1)
                elif kind == "FN":
                    for h in range(HALVES):
                        r = (HALVES * k + h) % OUT_RING
                        act.wait_ge(s_fn, 2 * CHUNKS * b + 2 * k + h + 1)
                        if type(b) is not int or CHUNKS * b + k > 0:
                            act.wait_ge(s_out[r], DMA * (CHUNKS * b + k))
                        nc.scalar.copy(out_sb[r][:], p.bank(job, h)[:]).then_inc(s_outc, 1)

            def norm_rows(p, f):
                act.wait_ge(s_rows, DMA * (FCHUNKS * p.b + f + 1))
                for i in range(4):
                    row = rows[:, i, 0:C]
                    a = nc.scalar.activation(row, row, ACT.Identity, bias=rows[:, i, C:C + 1],
                                             scale=rows[:, i, C + 1:C + 2])
                a.then_inc(s_cn, 1)

            def period(p):
                ffn = 0 in p.offsets
                if type(p.b) is int and p.b == -1:
                    act.wait_ge(s_wsplit, 2)
                if ffn:
                    norm_rows(p, 0)
                for s in range(STEPS):
                    if ffn and s % HB == 0:
                        f = s // HB
                        for h in range(HALVES):
                            act.wait_ge(s_xs, 2 * FCHUNKS * p.b + 2 * f + h + 1)
                            nc.scalar.copy(xs_hi[:, h, :], p.bank(("XS", 0, f), h)[:]).then_inc(s_xshi, 1)
                        if f + 1 < FCHUNKS:
                            act.dma_start(rows[:], x_table[p.q][(f + 1) * CHUNK:(f + 2) * CHUNK, :]
                                          .rearrange("(p i) c -> p i c", i=4)).then_inc(s_rows, DMA)
                    if s % HB == 0:
                        for job in p.jobs("ACT", 2 * s):
                            stage(p, job)
                    if ffn:
                        act.wait_ge(s_h, STEPS * p.b + s + 1)
                        bank, h = h_ps[s % 2], s % HB
                        nc.scalar.activation(g_hi[g_place(p.q, s)][:], bank[:], ACT.Gelu_apprx_tanh,
                                             bias=fb1[:, h:h + 1])
                        nc.scalar.activation(bank[:], bank[:], ACT.Gelu_apprx_tanh,
                                             bias=fb1[:, h:h + 1]).then_inc(s_g, 1)
                    if s % HB:
                        for job in p.jobs("ACT", 2 * s):
                            stage(p, job)
                    if ffn and s % HB == HB - 3 and s // HB + 1 < FCHUNKS:
                        norm_rows(p, s // HB + 1)
                    for job in p.jobs("ACT", 2 * s + 1):
                        stage(p, job)

            act.wait_ge(s_const, DMA * 12)
            run(act, period)

        @block.vector
        def _(dve):
            chain = {"before": 0, "here": 0}

            def mark(ins):
                chain["here"] += 1
                ins.then_inc(s_chain, 1)
                return chain["before"] + chain["here"]

            def link(ins):
                dve.wait_ge(s_chain, mark(ins))

            nc.vector.memset(ones_f[:], 1.0)
            nc.vector.memset(ones_sq, 1.0)
            nc.vector.memset(ones_row[:], 1.0)
            nc.vector.memset(ones_b[:], 1.0).then_inc(s_zero, 1)
            dve.wait_ge(s_const, DMA * 12)
            nc.vector.tensor_copy(tri[:], tri_f).then_inc(s_wsplit, 1)
            dve.wait_ge(s_rws, 1)
            link(nc.vector.tensor_scalar(rw_sum[:], small[:, RWS_COL:RWS_COL + 1], -1.0, None, ALU.mult))
            dve.wait_ge(s_wload, 2 * DMA)
            nc.vector.tensor_copy(w1_hi[:], w1_raw)
            link(nc.vector.tensor_copy(w2_hi[:], w2_raw))
            nc.vector.tensor_tensor(w1_lo[:], w1_raw, w1_hi[:].bitcast(F32), ALU.subtract)
            nc.vector.tensor_tensor(w2_lo[:], w2_raw, w2_hi[:].bitcast(F32), ALU.subtract).then_inc(s_wsplit, 1)

            def block_stats(n, b, q, pair):
                dve.wait_ge(s_copied[n], BLOCKS // 2 * b + pair + 1)
                for j in (2 * pair, 2 * pair + 1):
                    ins = nc.vector.bn_stats(stats[n][:, j, :], T[q][:, j, 0:C])
                if j == BLOCKS - 1:
                    stats_done[n] = mark(ins)

            stats_done = [0, 0]

            def newton(n, steps):
                a, v, u, r = norm_tmp[0][:], norm_tmp[2][:], norm_tmp[3][:], rstd[n][:]
                for _ in range(steps):
                    link(nc.vector.tensor_tensor(a, r, r, ALU.mult))
                    link(nc.vector.scalar_tensor_tensor(u, a, -0.5, v, ALU.mult, ALU.mult))
                    link(nc.vector.scalar_tensor_tensor(r, u, 1.5, r, ALU.add, ALU.mult))

            def moments(n, eps):
                a, d, v, u = (t[:] for t in norm_tmp)
                m, r, st = mean[n][:], rstd[n][:], stats[n]
                dve.wait_ge(s_chain, stats_done[n])
                nc.vector.tensor_tensor(d, st[:, :, 1], st[:, :, 4], ALU.subtract)
                nc.vector.tensor_tensor(a, st[:, :, 1], st[:, :, 4], ALU.add)
                link(nc.vector.tensor_tensor(v, st[:, :, 2], st[:, :, 5], ALU.add))
                nc.vector.tensor_scalar(m, a, 0.5, None, ALU.mult)
                link(nc.vector.tensor_tensor(u, d, d, ALU.mult))
                link(nc.vector.scalar_tensor_tensor(a, u, C / 4.0, v, ALU.mult, ALU.add))
                link(nc.vector.tensor_scalar(v, a, 1.0 / C, eps, ALU.mult, ALU.add))
                link(nc.vector.tensor_scalar(r.bitcast(I32), v.bitcast(I32), -0.5, 1597463007.0, ALU.mult, ALU.add))
                newton(n, 1)

            def digit_found(b, k):
                dve.wait_ge(s_tot, (ROUNDS + 1) * b + k + 1)
                link(nc.vector.tensor_scalar(junk[:], small[:, CNT_COL:CNT_COL + DIGITS], float(CHOSEN), None,
                                             ALU.is_ge, ALU.add, accum_out=passed[:]))
                link(nc.vector.scalar_tensor_tensor(base[(k + 1) % 2][:], passed[:], 16.0 ** (3 - k % 4),
                                                    base[k % 2][:], ALU.mult, ALU.add))

            def round_keys(b, q):
                lg = logit[q]
                dve.wait_ge(s_logit, CHUNKS * (b + 1))
                nc.vector.tensor_tensor(tmp[0][:], rstd[1][:], small[:, LOGIT_COL:LOGIT_COL + BLOCKS], ALU.mult)
                link(nc.vector.tensor_tensor(tmp[1][:], rstd[1][:], mean[1][:], ALU.mult))
                link(nc.vector.scalar_tensor_tensor(tmp[2][:], tmp[1][:], rw_sum[:, 0:1], tmp[0][:],
                                                    ALU.mult, ALU.add))
                link(nc.vector.tensor_scalar(lg[:], tmp[2][:], rb[:, 0:1], None, ALU.add))
                bits = lg[:].bitcast(I32)
                link(nc.vector.tensor_scalar(tmp[0][:].bitcast(I32), bits, 31, -2 ** 31,
                                             ALU.arith_shift_right, ALU.bitwise_or))
                link(nc.vector.tensor_tensor(tmp[1][:].bitcast(I32), bits, tmp[0][:].bitcast(I32), ALU.bitwise_xor))
                nc.vector.tensor_scalar(tmp[2][:].bitcast(U32), tmp[1][:].bitcast(U32), 16, None, ALU.logical_shift_right)
                link(nc.vector.tensor_scalar(key_lo[:], tmp[1][:].bitcast(U32), 0xFFFF, None, ALU.bitwise_and))
                nc.vector.memset(base[0][:], 0.0)
                link(nc.vector.tensor_copy(digit_key[:], tmp[2][:].bitcast(U32)))

            def stage(p, job):
                kind, off, k = job
                b, q = p.image(off)
                if kind == "N1":
                    block_stats(0, b, q, k)
                elif kind == "N2":
                    for i in range(2):
                        block_stats(1, b, q, 2 * k + i)
                elif kind == "N1M" and k == 0:
                    moments(0, EPS_C)
                elif kind == "N1M":
                    newton(0, 2)
                    nc.vector.scalar_tensor_tensor(offset1[:], mean[0][:], -1.0, rstd[0][:],
                                                   ALU.mult, ALU.mult).then_inc(s_mom, 1)
                elif kind == "NORM":
                    for j in (4 * k + 2, 4 * k + 3):
                        row = T[q][:, j, 0:C]
                        ins = nc.vector.tensor_scalar(row, row, mean[0][:, j:j + 1], rstd[0][:, j:j + 1],
                                                      ALU.subtract, ALU.mult)
                    ins.then_inc(s_norm[1], 1)
                elif kind == "SE1":
                    dve.wait_ge(s_pool, b + 1)
                    nc.vector.tensor_copy(pooled[:], small[:, POOL_COL:POOL_COL + HALVES]).then_inc(s_pooled, 1)
                elif kind == "SE2":
                    dve.wait_ge(s_hidr, b + 1)
                    nc.vector.tensor_scalar(hid4[:], group_mask[:], hid[:, 0:1], None, ALU.mult).then_inc(s_hid4, 1)
                elif kind == "SE3":
                    dve.wait_ge(s_se, b + 1)
                    nc.vector.tensor_tensor(
                        pre[:], small[:, SE_COL + 1:SE_COL + 1 + 2 * KGROUPS].rearrange("p (h k) -> p h k", h=HALVES),
                        cb2[:], ALU.add).then_inc(s_pre, 1)
                elif kind == "SE4":
                    dve.wait_ge(s_delta, b + 1)
                    nc.vector.tensor_scalar(coef[:, :, 0], delta[:, :, 0], 1.0, None, ALU.add)
                    nc.vector.tensor_copy(coef[:, :, 2], delta[:, :, 2])
                    link(nc.vector.tensor_scalar(coef[:, :, 1], delta[:, :, 1], 0.5, 1.0, ALU.mult, ALU.add))
                    nc.vector.scalar_tensor_tensor(coef[:, :, 3], delta[:, :, 3], 0.5, coef[:, :, 1],
                                                   ALU.mult, ALU.subtract).then_inc(s_coef, 1)
                elif kind == "CV":
                    for h in range(HALVES):
                        dve.wait_ge(s_branch, 2 * CHUNKS * b + 2 * k + h + 1)
                        nc.vector.scalar_tensor_tensor(branch[h][:], p.bank(job, h)[:], coef[:, h, 0:1],
                                                       branch[h][:], ALU.mult, ALU.max).then_inc(s_max, 1)
                    for h in range(HALVES):
                        at = X[:, h, tokens(k)]
                        dve.wait_ge(s_max, 2 * CHUNKS * b + 2 * k + h + 1)
                        nc.vector.scalar_tensor_tensor(at, branch[h][:], coef[:, h, 1:2], at,
                                                       ALU.add, ALU.add).then_inc(s_x2, 1)
                elif kind == "N2M" and k == 0:
                    moments(1, EPS_T)
                elif kind == "N2M" and k == 1:
                    newton(1, 2)
                elif kind == "N2M" and k == 2:
                    m, r, inv = mean[1][:], rstd[1][:], norm_tmp[0][:]
                    nc.vector.scalar_tensor_tensor(z_offset[:], m, -1.0, r, ALU.mult, ALU.mult)
                    link(nc.vector.tensor_scalar(z_scale[:], r, 1.0, None, ALU.add))
                    link(nc.vector.reciprocal(inv, z_scale[:]))
                    link(nc.vector.tensor_tensor(T[q][:, :, C + 1], r, inv, ALU.mult))
                    nc.vector.scalar_tensor_tensor(T[q][:, :, C], m, -1.0, T[q][:, :, C + 1], ALU.mult, ALU.mult)
                elif kind == "N2M":
                    round_keys(b, q)
                elif kind == "TK":
                    if k:
                        digit_found(b, k - 1)
                    if k == ROUNDS // 2:
                        nc.vector.tensor_scalar(tmp[1][:], digit_key[:], base[0][:, 0:1], 70000.0,
                                                ALU.is_gt, ALU.mult)
                        link(nc.vector.tensor_scalar(tmp[0][:], digit_key[:], base[0][:, 0:1], None, ALU.is_equal))
                        link(nc.vector.scalar_tensor_tensor(tmp[2][:], key_lo[:], 1.0, tmp[0][:],
                                                            ALU.add, ALU.mult))
                        nc.vector.tensor_tensor(low_key[:], tmp[2][:], tmp[1][:], ALU.add)
                        link(nc.vector.memset(base[0][:], 1.0))
                    src = digit_key if k < ROUNDS // 2 else low_key
                    link(nc.vector.scalar_tensor_tensor(
                        above[:], src[:].unsqueeze(1).to_broadcast([P, DIGITS, BLOCKS]), base[k % 2][:, 0:1],
                        digits[:, k % 4, :].unsqueeze(2).to_broadcast([P, DIGITS, BLOCKS]),
                        ALU.subtract, ALU.is_ge))
                    with nc.allow_low_precision("counts up to 32 are exact in bfloat16"):
                        nc.vector.tensor_reduce(count[:], above[:], AX_X, ALU.add).then_inc(s_cnt, 1)
                    for j in range(4 * k, 4 * k + 4):
                        row = T[q][:, j, 0:C]
                        nc.vector.tensor_scalar(row, row, z_scale[:, j:j + 1], z_offset[:, j:j + 1],
                                                ALU.mult, ALU.add)
                elif kind == "RANK1":
                    digit_found(b, ROUNDS - 1)
                    nc.vector.tensor_scalar(gt_eq[:, 0, :], low_key[:], base[0][:, 0:1], None, ALU.is_gt)
                    nc.vector.tensor_scalar(gt_eq[:, 1, :], low_key[:], base[0][:, 0:1], None,
                                            ALU.is_equal).then_inc(s_cnt, 1)
                elif kind == "RANK2" and k == 0:
                    dve.wait_ge(s_tot, (ROUNDS + 1) * (b + 1))
                    for i in range(2):
                        n = RANK_COL + (2 + i) * BLOCKS
                        ins = nc.vector.tensor_tensor_scan(incl[i][:], ones_row[:], small[:, n:n + BLOCKS], 0.0,
                                                           ALU.mult, ALU.add)
                    link(ins)
                    nc.vector.tensor_scalar(need[:], incl[0][:, BLOCKS - 1:BLOCKS], -1.0, float(CHOSEN),
                                            ALU.mult, ALU.add)
                    for i in range(2):
                        n = RANK_COL + (2 + i) * BLOCKS
                        ins = nc.vector.tensor_tensor(tmp[i][:], incl[i][:], small[:, n:n + BLOCKS], ALU.subtract)
                    link(ins)
                    for i in range(2):
                        n = RANK_COL + i * BLOCKS
                        ins = nc.vector.tensor_tensor(before[i][:], tmp[i][:], small[:, n:n + BLOCKS], ALU.add)
                    ins.then_inc(s_before, 1)
                    dve.wait_ge(s_before, b + 1)
                elif kind == "RANK2":
                    nc.vector.scalar_tensor_tensor(tmp[0][:], before[1][:], need[:, 0:1], gt_eq[:, 1, :],
                                                   ALU.is_lt, ALU.mult)
                    link(nc.vector.scalar_tensor_tensor(tmp[1][:], before[1][:], need[:, 0:1], before[0][:],
                                                        ALU.min, ALU.add))
                    link(nc.vector.tensor_tensor(chosen[:], tmp[0][:], gt_eq[:, 0, :], ALU.add))
                    nc.vector.tensor_tensor(logit[q][:], logit[q][:], chosen[:], ALU.mult)
                    link(nc.vector.tensor_scalar(tmp[2][:], chosen[:], -float(TOKENS), float(TOKENS),
                                                 ALU.mult, ALU.add))
                    nc.vector.tensor_tensor(index[q][:], tmp[2][:], tmp[1][:], ALU.add).then_inc(s_index, 1)
                    dve.wait_ge(s_index, b + 1)
                elif kind == "FN":
                    dve.wait_ge(s_back[k % 2], DMA * 4 * (CHUNKS // 2 * b + k // 2 + 1))
                    for j in range(4 * k, 4 * k + 4):
                        row = T[q][:, j, 0:C]
                        ins = nc.vector.scalar_tensor_tensor(row, y_back[:, 4 * (k % 2) + j % 4, :],
                                                             logit[q][:, j:j + 1], row, ALU.mult, ALU.add)
                    ins.then_inc(s_added, 1)

            def copy_y(b, q, f):
                dve.wait_ge(s_mm2, FCHUNKS * b + f + 1)
                if type(b) is not int or FCHUNKS * b + f > 0:
                    dve.wait_ge(s_ytab[(f - 1) % FCHUNKS], DMA * (b + (1 if f else 0)))
                for i in range(2):
                    ins = nc.vector.tensor_tensor(
                        y_rows[:, 2 * i:2 * i + 2, :], y_ps[i][:].rearrange("p (j c) -> p j c", j=2),
                        fb2[:].unsqueeze(1).to_broadcast([P, 2, C]), ALU.add)
                ins.then_inc(s_y, 1)

            def period(p):
                ffn = 0 in p.offsets
                if p.full:
                    chain.setdefault("first", chain["before"] + chain["here"])
                    chain["before"] = chain["first"] + chain.get("each", 0) * (p.b - FIRST_FULL)
                    chain["here"] = 0
                elif p.b == IMAGES - 2:
                    chain["before"], chain["here"] = chain["first"] + chain["each"] * N_FULL, 0
                for s in range(STEPS):
                    if ffn and s % HB == 0:
                        for h in range(HALVES):
                            dve.wait_ge(s_xshi, 2 * FCHUNKS * p.b + 2 * (s // HB) + h + 1)
                            nc.vector.tensor_tensor(xs_lo[:, h, :], p.bank(("XS", 0, s // HB), h)[:],
                                                    xs_hi[:, h, :].bitcast(F32), ALU.subtract).then_inc(s_xslo, 1)
                    for job in p.jobs("DVE", 2 * s):
                        stage(p, job)
                    if ffn:
                        dve.wait_ge(s_g, STEPS * p.b + s + 1)
                        r = g_place(p.q, s)
                        nc.vector.tensor_tensor(g_lo[r][:], h_ps[s % 2][:], g_hi[r][:].bitcast(F32),
                                                ALU.subtract).then_inc(s_glo, 1)
                    for job in p.jobs("DVE", 2 * s + 1):
                        stage(p, job)
                    if s % HB == 1 and (0 if s > HB else -1) in p.offsets:
                        copy_y(*p.image(0 if s > HB else -1), (s // HB - 1) % FCHUNKS)
                if p.full:
                    chain["each"] = chain["here"]

            run(dve, period)


def kernel(x, L0_conv_w1, L0_conv_b1, L0_conv_w2, L0_conv_b2, L0_ffn_attention_mask, L0_ffn_wr, L0_ffn_br,
           L0_ffn_w1, L0_ffn_b1, L0_ffn_w2, L0_ffn_b2):
    import concourse.bacc as bacc
    import numpy as np
    from concourse.bass_utils import run_bass_kernel_spmd

    images, channels, height, width = x.shape
    relu_h = L0_conv_w1.shape[0]
    groups = P // relu_h
    a = {k: np.asarray(v) for k, v in (
        ("w1", L0_conv_w1), ("b1", L0_conv_b1), ("w2", L0_conv_w2), ("b2", L0_conv_b2), ("wr", L0_ffn_wr),
        ("br", L0_ffn_br), ("f1", L0_ffn_w1), ("fb1", L0_ffn_b1), ("f2", L0_ffn_w2), ("fb2", L0_ffn_b2))}
    digits = 15
    consts = np.zeros((P, 2 * P + 4 * digits + groups), np.float32)
    consts[:, 0:P] = np.eye(P)
    consts[:, P:2 * P] = np.triu(np.ones((P, P)), 1)
    consts[:, 2 * P:2 * P + 4 * digits] = np.outer([4096, 256, 16, 1], np.arange(1, digits + 1)).reshape(-1)
    consts[:, 2 * P + 4 * digits:] = np.kron(np.eye(groups), np.ones((relu_h, 1)))
    arrays = {
        "x": np.asarray(x).reshape(images, channels, height * width),
        "conv_w1": np.tile(a["w1"].T, (1, groups)),
        "conv_b1": np.tile(a["b1"], groups)[:, None],
        "conv_w2": a["w2"].reshape(2, channels, 2, relu_h).transpose(0, 2, 3, 1).reshape(P, channels),
        "conv_b2": a["b2"].reshape(2, channels // P, P, 2).transpose(2, 1, 0, 3).reshape(P, -1, groups),
        "router_w": a["wr"].reshape(-1, P).T,
        "router_b": np.tile(a["br"], P)[:, None],
        "ffn_w1": a["f1"],
        "ffn_b1": a["fb1"].reshape(-1, P).T,
        "ffn_w2": a["f2"],
        "ffn_b2": np.tile(a["fb2"], (P, 1)),
        "consts": consts,
    }
    arrays = {k: np.ascontiguousarray(v) for k, v in arrays.items()}
    from concourse import mybir as _mybir

    nc = bacc.Bacc("TRN2", target_bir_lowering=False, num_devices=1, dynamic_dma_scratch_size=4096)
    args = {k: nc.dram_tensor(k, v.shape, _mybir.dt.from_np(v.dtype), kind="ExternalInput").ap()
            for k, v in arrays.items()}
    out = nc.dram_tensor("out", arrays["x"].shape, F32, kind="ExternalOutput").ap()
    metaformer_kernel(nc, out=out, **args)
    r = run_bass_kernel_spmd(nc, [arrays], core_ids=[0])
    return r.results[0]["out"].reshape(images, channels, height, width)
```
